# Optimizing a Trainium2 kernel written in Bass

```python
import numpy as np
import jax
import jax.numpy as jnp

def _softmax(x, axis=-1):
    return jax.nn.softmax(x, axis=axis)

def _gelu(x):
    return jax.nn.gelu(x, approximate=True)

def _silu(x):
    return jax.nn.silu(x)

def _sigmoid(x):
    return jax.nn.sigmoid(x)

def _layernorm(x, axis=-1, eps=1e-05):
    m = jnp.mean(x, axis=axis, keepdims=True)
    v = jnp.var(x, axis=axis, keepdims=True)
    return (x - m) / jnp.sqrt(v + eps)

def _scatter_add(tgt, idx, src, axis=0):
    return tgt.at[idx].add(src)

def _segment_sum(src, seg, n):
    return jax.ops.segment_sum(src, seg, n)
kernel_name = 'mk_flamingo_gated_d1_seqx_r8_1fc653'

def setup_inputs(seed: int=0):
    np.random.seed(seed)
    _w = jnp.asarray

    def _rec_inputs():
        import jax
        import jax.numpy as jnp
        _rk = jax.random.key(seed)
        x = -0.0002928 + 1 * jax.random.normal(jax.random.fold_in(_rk, 1), (8, 256, 128), jnp.float32)
        _lenS = 256 - jax.random.randint(jax.random.fold_in(_rk, 7), (8,), 0, max(1, 256 // 4) + 1, jnp.int32)
        _lenS2 = 256 - jax.random.randint(jax.random.fold_in(_rk, 8), (8,), 0, max(1, 256 // 4) + 1, jnp.int32)
        _ctx_512P = jax.random.normal(jax.random.fold_in(_rk, 11), (8, 16, 64), jnp.float32)
        _ctx_512c = jax.random.dirichlet(jax.random.fold_in(_rk, 511), 0.3 * jnp.ones((16,), jnp.float32), (8, 256))
        _ctx_512t = jnp.einsum('bsk,bkd->bsd', _ctx_512c, _ctx_512P)
        _ctx_512t = _ctx_512t * jax.lax.rsqrt(jnp.mean(jnp.square(_ctx_512t)) + 1e-12) * 0.953939
        ctx_512 = 0.00222621 + 0.99962 * (_ctx_512t + 0.3 * jax.random.normal(jax.random.fold_in(_rk, 611), (8, 256, 64), jnp.float32))
        _g = jax.random.normal(jax.random.fold_in(_rk, 9001), (2, 1), jnp.float32)
        _g = jnp.sign(_g) * jnp.maximum(jnp.abs(_g), 1.0) + (_g == 0) * 1.0
        g_xattn = _g[0]
        g_ffn = _g[1]
        return (x, ctx_512, g_xattn, g_ffn)
    x, ctx_512, g_xattn, g_ffn = _rec_inputs()

    def _L0_xattn_setup():
        import jax, jax.numpy as jnp
        import numpy as np
        B, T, TC, C, CC, H = (2, 256, 64, 128, 64, 16)
        D = C // H

        def _heads(t):
            b, l, _ = t.shape
            return t.reshape(b, l, H, D).transpose(0, 2, 1, 3)
        key = jax.random.key(seed)
        ks = jax.random.split(key, 18)
        w = lambda k, i, o: jax.random.normal(k, (i, o), jnp.float32) / np.sqrt(i).astype(np.float32)
        return {'x': jax.random.normal(ks[0], (B, T, C), jnp.float32), 'cross_input': jax.random.normal(ks[1], (B, TC, CC), jnp.float32), 'Wk': w(ks[2], C, C), 'bk': jnp.zeros((C,), jnp.float32), 'Wq': w(ks[3], C, C), 'bq': jnp.zeros((C,), jnp.float32), 'Wv': w(ks[4], C, C), 'bv': jnp.zeros((C,), jnp.float32), 'Wck': w(ks[5], CC, C), 'bck': jnp.zeros((C,), jnp.float32), 'Wcq': w(ks[6], C, C), 'bcq': jnp.zeros((C,), jnp.float32), 'Wcv': w(ks[7], CC, C), 'bcv': jnp.zeros((C,), jnp.float32), 'Wp': w(ks[8], C, C), 'bp': jnp.zeros((C,), jnp.float32)}
    _L0_xattn_all = _L0_xattn_setup()
    _L0_xattn_in = {k: v for k, v in _L0_xattn_all.items() if k in ('Wk', 'bk', 'Wq', 'bq', 'Wv', 'bv', 'Wck', 'bck', 'Wcq', 'bcq', 'Wcv', 'bcv', 'Wp', 'bp')}
    del _L0_xattn_all

    def _L0_ffn_setup():
        import jax, jax.numpy as jnp
        import numpy as np
        from jax import lax
        TOP_K = 4
        N_GROUP = 4
        TOPK_GROUP = 2
        ROUTED_SCALE = 2.5
        NEG_INF = -1000000000.0

        def _route(xf, router_weight, router_bias):
            T = xf.shape[0]
            E = router_weight.shape[0]
            logits = xf @ router_weight.T
            scores = jax.nn.sigmoid(logits)
            s_choice = scores + router_bias
            per_group = E // N_GROUP
            sg = s_choice.reshape(T, N_GROUP, per_group)
            group_scores = lax.top_k(sg, 2)[0].sum(-1)
            _, gidx = lax.top_k(group_scores, TOPK_GROUP)
            gmask = jnp.zeros((T, N_GROUP), dtype=bool).at[jnp.arange(T)[:, None], gidx].set(True)
            masked = jnp.where(gmask[:, :, None], sg, NEG_INF).reshape(T, E)
            _, topk_idx = lax.top_k(masked, TOP_K)
            w = jnp.take_along_axis(scores, topk_idx, axis=1)
            w = w / (w.sum(-1, keepdims=True) + 1e-20) * ROUTED_SCALE
            combine = jnp.zeros((T, E), dtype=xf.dtype).at[jnp.arange(T)[:, None], topk_idx].add(w)
            return combine
        key = jax.random.key(seed)
        ks = jax.random.split(key, 6)
        B, S, H, I, E = (2, 256, 128, 64, 16)
        x = jax.random.normal(ks[0], (B, S, H), dtype=jnp.float32)
        router_weight = jax.random.normal(ks[1], (E, H), dtype=jnp.float32) * 0.02
        router_bias = jnp.zeros((E,), dtype=jnp.float32)
        w_gate = jax.random.normal(ks[2], (E, I, H), dtype=jnp.float32) * 0.02
        w_up = jax.random.normal(ks[3], (E, I, H), dtype=jnp.float32) * 0.02
        w_down = jax.random.normal(ks[4], (E, H, I), dtype=jnp.float32) * 0.02
        return {'x': x, 'router_weight': router_weight, 'router_bias': router_bias, 'w_gate': w_gate, 'w_up': w_up, 'w_down': w_down}
    _L0_ffn_all = _L0_ffn_setup()
    _L0_ffn_in = {k: v for k, v in _L0_ffn_all.items() if k in ('router_weight', 'router_bias', 'w_gate', 'w_up', 'w_down')}
    del _L0_ffn_all
    return {'x': x, 'ctx_512': ctx_512, 'g_xattn': g_xattn, 'g_ffn': g_ffn, 'L0_xattn_Wk': _L0_xattn_in['Wk'], 'L0_xattn_bk': _L0_xattn_in['bk'], 'L0_xattn_Wq': _L0_xattn_in['Wq'], 'L0_xattn_bq': _L0_xattn_in['bq'], 'L0_xattn_Wv': _L0_xattn_in['Wv'], 'L0_xattn_bv': _L0_xattn_in['bv'], 'L0_xattn_Wck': _L0_xattn_in['Wck'], 'L0_xattn_bck': _L0_xattn_in['bck'], 'L0_xattn_Wcq': _L0_xattn_in['Wcq'], 'L0_xattn_bcq': _L0_xattn_in['bcq'], 'L0_xattn_Wcv': _L0_xattn_in['Wcv'], 'L0_xattn_bcv': _L0_xattn_in['bcv'], 'L0_xattn_Wp': _L0_xattn_in['Wp'], 'L0_xattn_bp': _L0_xattn_in['bp'], 'L0_ffn_router_weight': _L0_ffn_in['router_weight'], 'L0_ffn_router_bias': _L0_ffn_in['router_bias'], 'L0_ffn_w_gate': _L0_ffn_in['w_gate'], 'L0_ffn_w_up': _L0_ffn_in['w_up'], 'L0_ffn_w_down': _L0_ffn_in['w_down']}

def reference(x, ctx_512, g_xattn, g_ffn, L0_xattn_Wk, L0_xattn_bk, L0_xattn_Wq, L0_xattn_bq, L0_xattn_Wv, L0_xattn_bv, L0_xattn_Wck, L0_xattn_bck, L0_xattn_Wcq, L0_xattn_bcq, L0_xattn_Wcv, L0_xattn_bcv, L0_xattn_Wp, L0_xattn_bp, L0_ffn_router_weight, L0_ffn_router_bias, L0_ffn_w_gate, L0_ffn_w_up, L0_ffn_w_down):
    import jax
    import jax.numpy as jnp

    def _L0_xattn_ref(x, cross_input, Wk, bk, Wq, bq, Wv, bv, Wck, bck, Wcq, bcq, Wcv, bcv, Wp, bp):
        import jax, jax.numpy as jnp
        import numpy as np
        B, T, TC, C, CC, H = (2, 256, 64, 128, 64, 16)
        D = C // H

        def _heads(t):
            b, l, _ = t.shape
            return t.reshape(b, l, H, D).transpose(0, 2, 1, 3)
        scale = np.float32(1.0 / np.sqrt(D))
        q = _heads(x @ Wq + bq)
        k = _heads(x @ Wk + bk)
        v = _heads(x @ Wv + bv)
        att = jnp.einsum('bhqd,bhkd->bhqk', q, k) * scale
        causal = jnp.tril(jnp.ones((T, T), bool))
        att = jnp.where(causal[None, None], att, -jnp.inf)
        y = jnp.einsum('bhqk,bhkd->bhqd', jax.nn.softmax(att, axis=-1), v)
        qc = _heads(x @ Wcq + bcq)
        kc = _heads(cross_input @ Wck + bck)
        vc = _heads(cross_input @ Wcv + bcv)
        attc = jnp.einsum('bhqd,bhkd->bhqk', qc, kc) * scale
        y = y + jnp.einsum('bhqk,bhkd->bhqd', jax.nn.softmax(attc, axis=-1), vc)
        y = y.transpose(0, 2, 1, 3).reshape(x.shape[0], T, C)
        return y @ Wp + bp

    def _L0_ffn_ref(x, router_weight, router_bias, w_gate, w_up, w_down):
        import jax, jax.numpy as jnp
        import numpy as np
        from jax import lax
        TOP_K = 4
        N_GROUP = 4
        TOPK_GROUP = 2
        ROUTED_SCALE = 2.5
        NEG_INF = -1000000000.0

        def _route(xf, router_weight, router_bias):
            T = xf.shape[0]
            E = router_weight.shape[0]
            logits = xf @ router_weight.T
            scores = jax.nn.sigmoid(logits)
            s_choice = scores + router_bias
            per_group = E // N_GROUP
            sg = s_choice.reshape(T, N_GROUP, per_group)
            group_scores = lax.top_k(sg, 2)[0].sum(-1)
            _, gidx = lax.top_k(group_scores, TOPK_GROUP)
            gmask = jnp.zeros((T, N_GROUP), dtype=bool).at[jnp.arange(T)[:, None], gidx].set(True)
            masked = jnp.where(gmask[:, :, None], sg, NEG_INF).reshape(T, E)
            _, topk_idx = lax.top_k(masked, TOP_K)
            w = jnp.take_along_axis(scores, topk_idx, axis=1)
            w = w / (w.sum(-1, keepdims=True) + 1e-20) * ROUTED_SCALE
            combine = jnp.zeros((T, E), dtype=xf.dtype).at[jnp.arange(T)[:, None], topk_idx].add(w)
            return combine
        B, S, H = x.shape
        E = w_gate.shape[0]
        xf = x.reshape(-1, H)
        combine = _route(xf, router_weight, router_bias)
        out = jnp.zeros_like(xf)
        for e in range(E):
            g = xf @ w_gate[e].T
            u = xf @ w_up[e].T
            y_e = jax.nn.silu(g) * u @ w_down[e].T
            out = out + combine[:, e:e + 1] * y_e
        return out.reshape(B, S, H)
    x = x + jnp.tanh(g_xattn[0]) * _L0_xattn_ref(_layernorm(x, axis=-1), ctx_512, L0_xattn_Wk, L0_xattn_bk, L0_xattn_Wq, L0_xattn_bq, L0_xattn_Wv, L0_xattn_bv, L0_xattn_Wck, L0_xattn_bck, L0_xattn_Wcq, L0_xattn_bcq, L0_xattn_Wcv, L0_xattn_bcv, L0_xattn_Wp, L0_xattn_bp)
    x = x + jnp.tanh(g_ffn[0]) * _L0_ffn_ref(_layernorm(x, axis=-1), L0_ffn_router_weight, L0_ffn_router_bias, L0_ffn_w_gate, L0_ffn_w_up, L0_ffn_w_down)
    return x

_drawn_inputs = setup_inputs


def setup_inputs(seed=0):
    import zlib

    import numpy as np

    out = dict(_drawn_inputs(seed))
    spreads = {'L0_xattn_bk': (0.0, 0.8),
     'L0_xattn_bq': (0.0, 0.563),
     'L0_xattn_bv': (0.0, 0.1),
     'L0_xattn_bck': (0.0, 0.8),
     'L0_xattn_bcq': (0.0, 0.483),
     'L0_xattn_bcv': (0.0, 0.1),
     'L0_xattn_bp': (0.0, 0.1),
     'L0_ffn_router_bias': (0.0, 0.8)}
    factors = {'L0_ffn_router_weight': 8.0,
     'L0_ffn_w_gate': 8.0,
     'L0_ffn_w_up': 8.0,
     'L0_ffn_w_down': 8.0}
    for name, (base, spread) in spreads.items():
        noise = np.random.default_rng([zlib.crc32(name.encode()), seed]).standard_normal(out[name].shape)
        drawn = base * np.exp(spread * noise) if base else spread * noise
        out[name] = jnp.asarray(drawn.astype(out[name].dtype))
    for name, factor in factors.items():
        out[name] = (out[name] * factor).astype(out[name].dtype)
    return out
```

```python
import concourse.bass as bass
from concourse import mybir
from contextlib import ExitStack

FP32 = mybir.dt.float32
BF16 = mybir.dt.bfloat16
ALU = mybir.AluOpType
ACT = mybir.ActivationFunctionType
AX = mybir.AxisListType

B, T, C, CC, H, E, I = 8, 256, 128, 64, 16, 16, 64
D = C // H
NQ = T // 128
SCALE = D ** -0.5
EPS = 1e-5
NEG_INF = -1e9
MASKED = -1e30
PAD = -3e38
TAKEN = -2e38
TOP_GROUPS, TOP_EXPERTS, GROUPS = 2, 4, 4
ROUTED_SCALE = 2.5

PARTS = 3
STACK = PARTS * PARTS * D
SHIFT_ROW = STACK
VW = 32
SUM_COL = D

SELF, CROSS = 0, 1
NB = E * I // 128

S2_CHUNKS = []
S2_GROUP = []
for g in range(H // 4):
    S2_CHUNKS += [(SELF, 0, 4 * g, 2, 0), (SELF, 0, 4 * g + 2, 2, 0), (SELF, 1, 4 * g, 4, 128)]
    S2_GROUP += [g] * 3
for g in range(H // 4):
    S2_CHUNKS += [(CROSS, kt, 4 * g + hp, 2, 0) for kt in range(NQ) for hp in (0, 2)]
    S2_GROUP += [H // 4 + g] * 4
NC2 = len(S2_CHUNKS)
SELF_C2 = 3 * (H // 4)
LAST_CHUNK = [max(c for c in range(NC2) if S2_GROUP[c] == g) for g in range(8)]
PV_SLOT = [LAST_CHUNK[g] + 2 for g in range(8)]
NP = 7
assert NC2 % NP == 0 and NC2 % 2 == 0

S1_CHUNKS = [(SELF, 0, 4 * g, 4, 128) for g in range(4)] + [(SELF, 1, 2 * g, 2, 256) for g in range(8)]
S1_CHUNKS += [(CROSS, qt, 2 * g, 2, 256) for qt in range(NQ) for g in range(8)]
NC1 = len(S1_CHUNKS)
SELF_C1 = 12

SLOTS = NC2 + 3
M1_SLOTS = {}
for k in range(NC1 - SELF_C1):
    M1_SLOTS.setdefault(k // 2, []).append((0, SELF_C1 + k))
for k in range(SELF_C1):
    M1_SLOTS.setdefault(14 + k, []).append((1, k))
FFN_SLOT = [13, 15, 17, 18, 20, 22, 24, 26]
DOWN_SLOT = [20, 21, 22, 23, 24, 26, 28, 30]
RF = 4

MISC = [("y3", 0, -1), ("xnT", 1, 1), ("yT", 2, -1), ("qproj", 3, 1), ("wp", 4, -1), ("kproj", 5, 1),
        ("vproj", 6, 1), ("xn2T", 8, -1), ("shift_cross", 9, 0), ("route", 10, -1), ("y0", 11, 0), ("combT", 14, -1),
        ("y1", 16, 0), ("y2", 23, 0), ("shift_self", 26, 1)]
NMISC = len(MISC)
FIRST_TICK, LOOP_LO, LOOP_HI, LAST_TICK = -1, 1, 7, B


def on(b):
    return not isinstance(b, int) or 0 <= b < B


def misc_number(t, name):
    at = [m[0] for m in MISC].index(name)
    full = lambda u: [on(u + m[2]) for m in MISC]
    if isinstance(t, int):
        return sum(sum(full(u)) for u in range(FIRST_TICK, t)) + sum(full(t)[:at])
    before = sum(sum(full(u)) for u in range(FIRST_TICK, LOOP_LO))
    return (t - LOOP_LO) * NMISC + (before + at)


def misc_batch_number(b, name):
    off = dict((m[0], m[2]) for m in MISC)[name]
    return misc_number(b - off, name)


def build(nc, x, ctxT, w_model, w_ctx, cols, rows, w_pairs, w_down_in, out):
    stack = ExitStack()
    with stack:
        def sb(name, shape, dt=FP32):
            return stack.enter_context(nc.sbuf_tensor(name, shape, dt))

        def sem(name):
            return stack.enter_context(nc.semaphore(name))

        w_model_sb = sb("w_model_sb", [C, 5 * C + E])
        w_q, w_cq, w_k, w_v, w_p = (w_model_sb[:, n * C:(n + 1) * C] for n in range(5))
        w_router = w_model_sb[:, 5 * C:5 * C + E]
        w_ctx_sb = sb("w_ctx_sb", [CC, 2 * C])
        w_ck, w_cv = w_ctx_sb[:, 0:C], w_ctx_sb[:, C:2 * C]
        w_pairs_sb = sb("w_pairs_sb", [C, 2, E * I])
        w_gate, w_up = w_pairs_sb[:, 0, :], w_pairs_sb[:, 1, :]
        w_down = sb("w_down", [128, NB, C])
        cols_sb = sb("cols_sb", [C, 6])
        bias_q = sb("bias_q", [C, 2])
        bias_v = sb("bias_v", [C, 1])
        rows_sb = sb("rows_sb", [128, C + E + 2])
        rb_row, gates = rows_sb[:, C:C + E], rows_sb[:, C + E:C + E + 2]
        bp_row = sb("bp_row", [128, C])
        gate = sb("gate", [128, 3])
        minus_half = sb("minus_half", [128, NQ])
        ident = sb("ident", [128, 128])
        ident_b = sb("ident_b", [128, 128], BF16)
        causal = sb("causal", [128, 4, 128], BF16)
        zero_row = sb("zero_row", [H, 2 * T], BF16)
        ones_row = sb("ones_row", [H, 2 * T], BF16)

        x_in = sb("x_in", [128, 2, NQ, C])
        ctx_in = sb("ctx_in", [CC, 2, T])
        stats1, mean1, rstd1 = sb("stats1", [128, NQ, 6]), sb("mean1", [128, NQ, 2]), sb("rstd1", [128, NQ])
        xn = sb("xn", [128, NQ, C])
        xnT = sb("xnT", [C, T])
        proj = sb("proj", [C, 2, 2 * T])
        rest = sb("rest", [C, 2, 2 * T])
        part = sb("part", [C, 2, PARTS, 2 * T], BF16)
        q_stack = sb("q_stack", [128, 2, H, 2, T], BF16)
        k_stack = sb("k_stack", [128, 2, H, 2, T], BF16)
        v_ext = sb("v_ext", [128, 2, 2, NQ, H, VW])
        row_max = sb("row_max", [128, 2, NQ, H])
        shiftT = sb("shiftT", [H, 2, T], BF16)
        probs = sb("probs", [128, NP, 512])
        y_raw = sb("y_raw", [128, 2, 512])
        recip = sb("recip", [128, 16])
        y_tmp = sb("y_tmp", [128, NQ, C // 2])
        y = sb("y", [128, NQ, C])
        yT = sb("yT", [C, T])
        x_res = sb("x_res", [128, 2, NQ, C])
        x1 = sb("x1", [128, NQ, C])
        stats2, mean2, rstd2 = sb("stats2", [128, NQ, 6]), sb("mean2", [128, NQ, 2]), sb("rstd2", [128, NQ])
        xn2 = sb("xn2", [128, NQ, C])
        xn2T = sb("xn2T", [C, T])
        r_tanh, r_score, r_choice = (sb(n, [128, NQ, E]) for n in ("r_tanh", "r_score", "r_choice"))
        r_pair = sb("r_pair", [128, NQ * GROUPS, 6])
        r_gin, r_gout = sb("r_gin", [128, NQ, 10]), sb("r_gout", [128, NQ, 10])
        r_g8, r_gtop = sb("r_g8", [128, NQ, 8]), sb("r_gtop", [128, NQ, 8])
        r_gsel, r_gpen = sb("r_gsel", [128, NQ, GROUPS]), sb("r_gpen", [128, NQ, GROUPS])
        r_ein, r_eout = sb("r_ein", [128, NQ, 20]), sb("r_eout", [128, NQ, 20])
        r_e8, r_etop = sb("r_e8", [128, NQ, 8]), sb("r_etop", [128, NQ, 8])
        r_sel, r_w = sb("r_sel", [128, NQ, E]), sb("r_w", [128, NQ, E])
        r_sum = sb("r_sum", [128, NQ])
        combT = sb("combT", [E, T])
        comb = sb("comb", [128, NB, T])
        f_tanh, f_gate = sb("f_tanh", [128, T]), sb("f_gate", [128, T])
        f_h, f_hc = sb("f_h", [128, RF, T]), sb("f_hc", [128, RF, T])
        y_out = sb("y_out", [128, NQ, C])

        q_scr = nc.dram_tensor("q_scr", (2, PARTS, D, H, 2 * T), BF16).ap()
        k_scr = nc.dram_tensor("k_scr", (2, D, PARTS, H, 2 * T), BF16).ap()
        c_scr = nc.dram_tensor("c_scr", (E, T), FP32).ap()

        bank = [stack.enter_context(nc.psum_tensor(f"bank{n}", [128, 512], FP32)) for n in range(8)]
        max_bank, exp_bank, pv_bank, down_bank, gu_bank, misc = bank[0:2], bank[2:4], bank[4], bank[5], bank[6], bank[7]

        w_first = sem("w_first")
        w_rest = sem("w_rest")
        ones_in = sem("ones_in")
        v_cleared = sem("v_cleared")
        stack_cleared = sem("stack_cleared")
        const_made = sem("const_made")
        const_step = sem("const_step")
        scaled = sem("scaled")
        gate_made = sem("gate_made")
        x_loaded = sem("x_loaded")
        stats_done = sem("stats_done")
        rstd_done = sem("rstd_done")
        rstd_step = sem("rstd_step")
        xn_done = sem("xn_done")
        ln1_step = sem("ln1_step")
        split_step = sem("split_step")
        split_done = sem("split_done")
        part_stored = sem("part_stored")
        stack_in = sem("stack_in")
        res_done = sem("res_done")
        max_scores = sem("max_scores")
        max_taken = sem("max_taken")
        shift_in = [sem("shift_in_self"), sem("shift_in_cross")]
        exp_scores = sem("exp_scores")
        exp_done = sem("exp_done")
        mask_done = sem("mask_done")
        pv_done = sem("pv_done")
        pv_copied = sem("pv_copied")
        y_step = sem("y_step")
        y_done = sem("y_done")
        misc_ready = sem("misc_ready")
        misc_free = sem("misc_free")
        ln2_step = sem("ln2_step")
        stats2_done = sem("stats2_done")
        rstd2_done = sem("rstd2_done")
        rstd2_step = sem("rstd2_step")
        xn2_done = sem("xn2_done")
        route_step = sem("route_step")
        comb_done = sem("comb_done")
        comb_stored = sem("comb_stored")
        comb_in = sem("comb_in")
        gu_ready = sem("gu_ready")
        f_tanh_done = sem("f_tanh_done")
        f_gate_done = sem("f_gate_done")
        f_h_done = sem("f_h_done")
        f_hc_done = sem("f_hc_done")
        down_used = sem("down_used")
        out_done = sem("out_done")
        stored = sem("stored")
        pool_carrier, sp_carrier = sem("pool_carrier"), sem("sp_carrier")

        block = stack.enter_context(nc.Block())

        def ge(eng, s, v):
            if not isinstance(v, int) or v > 0:
                eng.wait_ge(s, v)

        def ticks(eng, tick):
            for t in range(FIRST_TICK, LOOP_LO):
                tick(t, t % 2)
            with eng.Fori(LOOP_LO, LOOP_HI, 2) as t:
                tick(t, LOOP_LO % 2)
                tick(t + 1, (LOOP_LO + 1) % 2)
            for t in range(LOOP_HI, LAST_TICK + 1):
                tick(t, t % 2)

        def misc_slot(name):
            return dict((m[0], m[1]) for m in MISC)[name]

        @block.sync
        def _(sp):
            def load_x(b, par):
                sp.dma_start(x_in[:, par], x[b].rearrange("(n p) c -> p n c", p=128)).then_inc(x_loaded, 16)
                sp.dma_start(ctx_in[:, par], ctxT[:, b]).then_inc(x_loaded, 16)

            load_x(0, 0)
            sp.dma_start(w_model_sb[:, :], w_model).then_inc(w_first, 16)
            sp.dma_start(w_ctx_sb[:, :], w_ctx).then_inc(w_first, 16)
            sp.dma_start(cols_sb[:, :], cols).then_inc(w_first, 16)
            sp.dma_start(rows_sb[:, :], rows.partition_broadcast(128)).then_inc(w_rest, 16)
            sp.dma_start(w_pairs_sb[:, :, :], w_pairs).then_inc(w_rest, 16)
            sp.dma_start(w_down[:, :, :], w_down_in).then_inc(w_rest, 16)

            def tick(t, par):
                if on(t + 2):
                    ge(sp, x_loaded, (t + 2) * 32)
                    sp.sem_inc(sp_carrier, 1)
                    ge(sp, res_done, t + 1)
                    sp.sem_inc(sp_carrier, 1)
                    if on(t):
                        ge(sp, misc_free, misc_number(t - 1, "vproj") + 1)
                    load_x(t + 2 if isinstance(t, int) else (t + 2) % B, par)
                if on(t):
                    ge(sp, misc_free, misc_number(t, "shift_cross") + 1)
                    sp.dma_start(q_stack[SHIFT_ROW:SHIFT_ROW + 1, par, :, CROSS, :], shiftT[:, CROSS, :]).then_inc(shift_in[CROSS], 16)
                if on(t + 1):
                    b, p1 = t + 1, 1 - par
                    for n in range(PARTS):
                        ge(sp, split_done, b * 6 + n + 1)
                        sp.dma_start(q_scr[p1, n].rearrange("d h x -> h d x"), part[:, 0, n, :]).then_inc(part_stored, 16)
                    ge(sp, pv_done, (b - 1) * 8)
                    sp.sem_inc(sp_carrier, 1)
                    if isinstance(b, int) and b < 2:
                        sp.wait_ge(stack_cleared, 2 * b + 2)
                        sp.dma_start(k_stack[SHIFT_ROW:SHIFT_ROW + 1, p1], ones_row[:, :]).then_inc(ones_in, 16)
                    ge(sp, part_stored, b * 96 + 48)
                    for n in range(PARTS):
                        src = q_scr[p1, n].rearrange("d h x -> d (h x)").unsqueeze(1).broadcast_to([D, PARTS, H * 2 * T])
                        sp.dma_start(q_stack[n * PARTS * D:(n + 1) * PARTS * D, p1], src).then_inc(stack_in, 16)
                    sp.dma_start(q_stack[SHIFT_ROW:SHIFT_ROW + 1, p1], zero_row[:, :]).then_inc(stack_in, 16)
                    for n in range(PARTS):
                        ge(sp, split_done, b * 6 + PARTS + n + 1)
                        sp.dma_start(k_scr[p1, :, n].rearrange("d h x -> h d x"), part[:, 1, n, :]).then_inc(part_stored, 16)
                    ge(sp, part_stored, b * 96 + 96)
                    for n in range(PARTS):
                        src = k_scr[p1].rearrange("d n h x -> (d n) (h x)")
                        sp.dma_start(k_stack[n * PARTS * D:(n + 1) * PARTS * D, p1], src).then_inc(stack_in, 16)
                    ge(sp, misc_free, misc_number(t, "shift_self") + 1)
                    sp.dma_start(q_stack[SHIFT_ROW:SHIFT_ROW + 1, p1, :, SELF, :], shiftT[:, SELF, :]).then_inc(shift_in[SELF], 16)
                if on(t - 1):
                    ge(sp, out_done, t)
                    sp.dma_start(out[t - 1].rearrange("(n p) c -> p n c", p=128), y_out[:, :, :]).then_inc(stored, 16)

            sp.sem_inc(stored, 16)
            ticks(sp, tick)
            sp.wait_ge(x_loaded, 32 * (LOOP_HI - 1 + 3))
            sp.wait_ge(stored, 16 * B + 16)
            sp.wait_ge(part_stored, 96 * B)
            sp.wait_ge(comb_stored, 16 * B)

        @block.gpsimd
        def _(pool):
            nc.gpsimd.memset(ident[:, :], 0.0).then_inc(const_step, 1)
            nc.gpsimd.memset(minus_half[:, :], -0.5).then_inc(const_step, 1)
            nc.gpsimd.memset(causal[:, :, :], 0.0).then_inc(const_step, 1)
            nc.gpsimd.memset(ident_b[:, :], 0.0).then_inc(const_step, 1)
            nc.gpsimd.memset(zero_row[:, :], 0.0).then_inc(const_step, 1)
            nc.gpsimd.memset(ones_row[:, :], 1.0).then_inc(const_step, 1)
            pool.wait_ge(const_step, 6)
            nc.gpsimd.affine_select(out=ident[:, :], in_=ident[:, :], compare_op=ALU.not_equal, fill=1.0, base=0,
                                    pattern=[[-1, 128]], channel_multiplier=1).then_inc(const_made, 1)
            nc.gpsimd.affine_select(out=ident_b[:, :], in_=ident_b[:, :], compare_op=ALU.not_equal, fill=1.0, base=0,
                                    pattern=[[-1, 128]], channel_multiplier=1).then_inc(const_made, 1)
            nc.gpsimd.affine_select(out=causal[:, :, :], in_=causal[:, :, :], compare_op=ALU.is_ge, fill=MASKED, base=0,
                                    pattern=[[0, 4], [-1, 128]], channel_multiplier=1).then_inc(const_made, 1)

            def clear_values():
                v = v_ext[:, :, :, :, :, :].rearrange("p a k n h v -> p (a k n h) v")
                nc.gpsimd.memset(v, 0.0).then_inc(const_step, 1)
                pool.wait_ge(const_step, 7)
                nc.gpsimd.memset(v[:, :, SUM_COL:SUM_COL + 1], 1.0).then_inc(v_cleared, 1)

            def rstd(mv, rs, ready, b, step, done):
                pool.wait_ge(ready, b + 1)
                pool.sem_inc(pool_carrier, 1)
                nc.gpsimd.tensor_scalar(rs[:, :], mv[:, :, 1], EPS, None, ALU.add).then_inc(step, 1)
                pool.wait_ge(step, 1)
                pool.sem_clear(step)
                nc.gpsimd.tensor_tensor(rs[:, :], rs[:, :], minus_half[:, :], ALU.pow).then_inc(done, 1)

            def split(t, b, kind):
                src, rem = proj[:, kind, :], rest[:, kind, :]
                prt = part[:, kind]
                n = b * 6 + 3 * kind
                pool.wait_ge(misc_free, misc_number(t, ("qproj", "kproj")[kind]) + 1)
                ge(pool, part_stored, b * 96 - 48 + 48 * kind)
                pool.sem_inc(pool_carrier, 1)
                nc.gpsimd.tensor_scalar(prt[:, 0, :], src, 1.0, None, ALU.mult).then_inc(split_done, 1)
                pool.wait_ge(split_done, n + 1)
                nc.gpsimd.tensor_tensor(rem, src, prt[:, 0, :], ALU.subtract).then_inc(split_step, 1)
                pool.wait_ge(split_step, 1)
                pool.sem_clear(split_step)
                nc.gpsimd.tensor_scalar(prt[:, 1, :], rem, 1.0, None, ALU.mult).then_inc(split_done, 1)
                pool.wait_ge(split_done, n + 2)
                nc.gpsimd.tensor_tensor(prt[:, 2, :], rem, prt[:, 1, :], ALU.subtract).then_inc(split_done, 1)

            def mask(b, s):
                _, kt, h0, nh, q0 = S2_CHUNKS[s]
                pool.wait_ge(exp_done, b * NC2 + s + 1)
                pool.sem_inc(pool_carrier, 1)
                p = probs[:, s % NP, :].rearrange("p (h q) -> p h q", h=nh)[:, :, 0:128]
                nc.gpsimd.affine_select(out=p, in_=p, compare_op=ALU.is_ge, fill=0.0, base=0,
                                        pattern=[[0, nh], [1, 128]], channel_multiplier=-1).then_inc(mask_done, 1)

            def spread_weights(t, b):
                pool.wait_ge(misc_free, misc_number(t, "combT") + 1)
                pool.sem_inc(pool_carrier, 1)
                pool.dma_start(c_scr, combT[:, :]).then_inc(comb_stored, 16)
                pool.wait_ge(comb_stored, b * 16 + 16)
                pool.sem_inc(pool_carrier, 1)
                for e2 in range(2):
                    src = c_scr.rearrange("(j e) t -> e j t", e=2)[e2].partition_broadcast(I)
                    pool.dma_start(comb[e2 * I:(e2 + 1) * I, :, :], src).then_inc(comb_in, 16)

            def combine(b, j):
                pool.wait_ge(f_h_done, b * NB + j + 1)
                if j == 0:
                    pool.wait_ge(comb_in, b * 32 + 32)
                if j >= RF:
                    pool.wait_ge(down_used, b * NB + j + 1 - RF)
                nc.gpsimd.tensor_tensor(f_hc[:, j % RF, :], f_h[:, j % RF, :], comb[:, j, :], ALU.mult).then_inc(f_hc_done, 1)

            def tick(t, par):
                for s in range(SLOTS):
                    if s == 0 and on(t + 1):
                        rstd(mean1, rstd1, stats_done, t + 1, rstd_step, rstd_done)
                        if isinstance(t, int) and t == FIRST_TICK:
                            clear_values()
                    if on(t) and s < SELF_C2:
                        mask(t, s)
                    if s == 4 and on(t + 1):
                        split(t, t + 1, 0)
                    if s == 7 and on(t + 1):
                        split(t, t + 1, 1)
                    if s == 6 and on(t - 1):
                        rstd(mean2, rstd2, stats2_done, t - 1, rstd2_step, rstd2_done)
                    if s == 12 and on(t + 1):
                        b, p1 = t + 1, 1 - par
                        pool.wait_ge(x_loaded, b * 32 + 32)
                        if isinstance(t, int) and t == FIRST_TICK:
                            pool.wait_ge(gate_made, 3)
                        if on(b - 2):
                            ge(pool, misc_free, misc_number(t, "wp") + 1)
                        nc.gpsimd.tensor_tensor(x_res[:, p1], x_in[:, p1],
                                                bp_row[:, :].unsqueeze(1).broadcast_to([128, NQ, C]), ALU.add).then_inc(res_done, 1)
                    if s == misc_slot("combT") and on(t - 1):
                        spread_weights(t, t - 1)
                    for j in range(NB):
                        if s == max(FFN_SLOT[j] + 1, 15) and on(t - 1):
                            combine(t - 1, j)

            ticks(pool, tick)

        @block.scalar
        def _(act):
            act.wait_ge(w_rest, 48)
            nc.scalar.activation(gate[:, 0:2], gates, ACT.Tanh).then_inc(gate_made, 1)
            act.wait_ge(scaled, 1)

            def take(t, name):
                act.wait_ge(misc_ready, misc_number(t, name) + 1)

            def evacuate_pv(b, i):
                act.wait_ge(pv_done, b * 8 + 2 * i + 2)
                prev = misc_batch_number(b, f"y{i - 2}") if i >= 2 else misc_batch_number(b - 1, f"y{i + 2}")
                if i >= 2 or on(b - 1):
                    ge(act, misc_ready, prev + 1)
                nc.scalar.activation(y_raw[:, i % 2, :], pv_bank[:, :], ACT.Copy).then_inc(pv_copied, 1)

            def tick(t, par):
                p1 = 1 - par
                for s in range(SLOTS):
                    if on(t) and s < NC2:
                        act.wait_ge(exp_scores, t * NC2 + s + 1)
                        old = s - NP
                        if old >= 0:
                            act.wait_ge(pv_done, t * 8 + S2_GROUP[old] + 1)
                        else:
                            ge(act, pv_done, (t - 1) * 8 + S2_GROUP[old + NC2] + 1 if not isinstance(t, int) or t > 0 else 0)
                        nc.scalar.activation(probs[:, s % NP, :], exp_bank[s % 2][:, :], ACT.Exp).then_inc(exp_done, 1)
                    for j in range(NB):
                        if s == FFN_SLOT[j] and on(t - 1):
                            b = t - 1
                            act.wait_ge(gu_ready, b * NB + j + 1)
                            if j:
                                act.wait_ge(f_gate_done, b * NB + j)
                            nc.scalar.activation(f_tanh[:, :], gu_bank[:, 0:T], ACT.Tanh, scale=0.5).then_inc(f_tanh_done, 1)
                    if s == misc_slot("xnT") and on(t + 1):
                        take(t, "xnT")
                        nc.scalar.activation(xnT[:, :], misc[:, 0:T], ACT.Copy).then_inc(misc_free, 1)
                    if s == misc_slot("yT") and on(t - 1):
                        take(t, "yT")
                        nc.scalar.activation(yT[:, :], misc[:, 0:T], ACT.Identity, bias=bias_v[:, :]).then_inc(misc_free, 1)
                    if s == misc_slot("qproj") and on(t + 1):
                        take(t, "qproj")
                        ge(act, split_done, (t + 1) * 6)
                        nc.scalar.activation(proj[:, 0, 0:T], misc[:, 0:T], ACT.Identity, bias=bias_q[:, 0:1], scale=SCALE)
                        nc.scalar.activation(proj[:, 0, T:2 * T], misc[:, T:2 * T], ACT.Identity, bias=bias_q[:, 1:2],
                                             scale=SCALE).then_inc(misc_free, 1)
                    if s == misc_slot("kproj") and on(t + 1):
                        take(t, "kproj")
                        nc.scalar.activation(proj[:, 1, 0:T], misc[:, 0:T], ACT.Identity, bias=cols_sb[:, 2:3])
                        nc.scalar.activation(proj[:, 1, T:2 * T], misc[:, T:2 * T], ACT.Identity,
                                             bias=cols_sb[:, 3:4]).then_inc(misc_free, 1)
                    if s == misc_slot("vproj") and on(t + 1):
                        take(t, "vproj")
                        act.wait_ge(v_cleared, 1)
                        for kind in (SELF, CROSS):
                            last = nc.scalar.activation(
                                v_ext[:, p1, kind, :, :, 0:D],
                                misc[:, kind * T:(kind + 1) * T].rearrange("p (n h d) -> p n h d", n=NQ, d=D), ACT.Copy)
                        last.then_inc(misc_free, 1)
                    if s == misc_slot("xn2T") and on(t - 1):
                        take(t, "xn2T")
                        nc.scalar.activation(xn2T[:, :], misc[:, 0:T], ACT.Copy).then_inc(misc_free, 1)
                    if s == misc_slot("route") and on(t - 1):
                        take(t, "route")
                        nc.scalar.activation(r_tanh[:, :, :], misc[:, 0:NQ * E].rearrange("p (n e) -> p n e", n=NQ), ACT.Tanh,
                                             scale=0.5).then_inc(misc_free, 1)
                    if s == misc_slot("combT") and on(t - 1):
                        take(t, "combT")
                        nc.scalar.activation(combT[:, :], misc[0:E, 0:T], ACT.Copy).then_inc(misc_free, 1)
                    for i in range(4):
                        if s == PV_SLOT[2 * i + 1] and on(t):
                            evacuate_pv(t, i)

            ticks(act, tick)

        @block.tensor
        def _(pe):
            pe.wait_ge(w_first, 48)
            pe.wait_ge(const_made, 3)
            pe.wait_ge(w_rest, 48)

            def max_chunk(b, par, k):
                kind, qt, h0, nh, keys = S1_CHUNKS[k]
                if k == 0:
                    pe.wait_ge(stack_in, b * 112 + 112)
                    if isinstance(b, int) and b < 2:
                        pe.wait_ge(ones_in, 16 * b + 16)
                ge(pe, max_taken, b * NC1 + k - 1)
                ps = max_bank[k % 2][:, :].rearrange("p (h k) -> p h k", h=nh)
                if kind == SELF:
                    pe.matmul(ps[:, :, keys - 128:keys], ident_b[:, :], causal[:, 0:nh, :], start=True, stop=False)
                for n in range(nh):
                    h = h0 + n
                    q = q_stack[:, par, h, kind, qt * 128:(qt + 1) * 128]
                    if kind == SELF:
                        for kt in range(keys // 128):
                            last = pe.matmul(ps[:, n, kt * 128:(kt + 1) * 128], q, k_stack[:, par, h, kind, kt * 128:(kt + 1) * 128],
                                             start=False, stop=n == nh - 1 and kt == keys // 128 - 1)
                    else:
                        last = pe.matmul(ps[:, n, :], q, k_stack[:, par, h, kind, :], start=n == 0, stop=n == nh - 1)
                last.then_inc(max_scores, 1)

            def exp_chunk(t, par, s):
                kind, kt, h0, nh, q0 = S2_CHUNKS[s]
                if s == 0:
                    pe.wait_ge(shift_in[SELF], t * 16 + 16)
                if s == SELF_C2:
                    pe.wait_ge(shift_in[CROSS], t * 16 + 16)
                ge(pe, exp_done, t * NC2 + s - 1)
                ps = exp_bank[s % 2][:, :].rearrange("p (h q) -> p h q", h=nh)
                for n in range(nh):
                    h = h0 + n
                    last = pe.matmul(ps[:, n, :], k_stack[:, par, h, kind, kt * 128:(kt + 1) * 128],
                                     q_stack[:, par, h, kind, q0:T], start=n == 0, stop=n == nh - 1)
                last.then_inc(exp_scores, 1)

            def weigh_values(t, par, g):
                kind, g4 = divmod(g, 4)
                pe.wait_ge(exp_done, t * NC2 + LAST_CHUNK[g] + 1)
                if kind == SELF:
                    pe.wait_ge(mask_done, t * SELF_C2 + 3 * g4 + 3)
                if g % 2 == 0:
                    ge(pe, pv_copied, t * 4 + g // 2)
                col = (g % 2) * T
                for kt in range(NQ):
                    for n in range(4):
                        chunk, at = [(c, h0) for c, (kd, k_, h0, nh, q0) in enumerate(S2_CHUNKS)
                                     if kd == kind and k_ == kt and h0 <= 4 * g4 + n < h0 + nh][0]
                        nh, q0 = S2_CHUNKS[chunk][3:]
                        p = probs[:, chunk % NP, :].rearrange("p (h q) -> p h q", h=nh)[:, 4 * g4 + n - at, :]
                        last = pe.matmul(pv_bank[32 * n:32 * n + VW, col + q0:col + T], v_ext[:, par, kind, kt, 4 * g4 + n, :], p,
                                         start=kt == 0, stop=kt == NQ - 1, tile_position=(0, 32 * n))
                last.then_inc(pv_done, 1)

            def own(t, name):
                ge(pe, misc_free, misc_number(t, name))

            def transposes(dst, src):
                for n in range(NQ):
                    last = pe.transpose(dst[:, n * 128:(n + 1) * 128], src(n), ident[:, :])
                return last

            def misc_use(t, par, name, off):
                b, p1 = t + off, 1 - par
                own(t, name)
                if name == "xnT":
                    pe.wait_ge(xn_done, b + 1)
                    last = transposes(misc, lambda n: xn[:, n, :])
                elif name == "qproj":
                    pe.wait_ge(misc_free, misc_number(t, "xnT") + 1)
                    pe.matmul(misc[:, 0:T], w_q, xnT[:, :], start=True, stop=True)
                    last = pe.matmul(misc[:, T:2 * T], w_cq, xnT[:, :], start=True, stop=True)
                elif name == "kproj":
                    pe.wait_ge(x_loaded, b * 32 + 32)
                    pe.matmul(misc[:, 0:T], w_k, xnT[:, :], start=True, stop=True)
                    last = pe.matmul(misc[:, T:2 * T], w_ck, ctx_in[:, p1, :], start=True, stop=True)
                elif name == "vproj":
                    for n in range(NQ):
                        pe.matmul(misc[:, n * 128:(n + 1) * 128], xnT[:, n * 128:(n + 1) * 128], w_v, start=True, stop=True)
                    for n in range(NQ):
                        last = pe.matmul(misc[:, T + n * 128:T + (n + 1) * 128], ctx_in[:, p1, n * 128:(n + 1) * 128], w_cv,
                                         start=True, stop=True)
                elif name in ("shift_cross", "shift_self"):
                    kind = CROSS if name == "shift_cross" else SELF
                    pe.wait_ge(max_taken, b * NC1 + (NC1 if kind == CROSS else SELF_C1))
                    for n in range(NQ):
                        last = pe.transpose(misc[0:H, n * 128:(n + 1) * 128], row_max[:, kind, n, :], ident[:, :])
                elif name in ("y0", "y1", "y2", "y3"):
                    i = int(name[1])
                    pe.wait_ge(pv_copied, b * 4 + i + 1)
                    for qt in range(NQ):
                        for g in range(2):
                            last = pe.transpose(misc[:, (qt * 2 + g) * 128:(qt * 2 + g + 1) * 128],
                                                y_raw[:, i % 2, g * T + qt * 128:g * T + (qt + 1) * 128], ident[:, :])
                elif name == "yT":
                    pe.wait_ge(y_done, b + 1)
                    last = transposes(misc, lambda n: y[:, n, :])
                elif name == "wp":
                    pe.wait_ge(misc_free, misc_number(t, "yT") + 1)
                    for n in range(NQ):
                        last = pe.matmul(misc[:, n * 128:(n + 1) * 128], yT[:, n * 128:(n + 1) * 128], w_p, start=True, stop=True)
                elif name == "xn2T":
                    pe.wait_ge(xn2_done, b + 1)
                    last = transposes(misc, lambda n: xn2[:, n, :])
                elif name == "route":
                    pe.wait_ge(misc_free, misc_number(t, "xn2T") + 1)
                    for n in range(NQ):
                        last = pe.matmul(misc[:, n * E:(n + 1) * E], xn2T[:, n * 128:(n + 1) * 128], w_router, start=True, stop=True)
                elif name == "combT":
                    pe.wait_ge(comb_done, b + 1)
                    for n in range(NQ):
                        last = pe.transpose(misc[0:E, n * 128:(n + 1) * 128], r_w[:, n, :], ident[:, :])
                last.then_inc(misc_ready, 1)

            def gate_up(b, j):
                if j:
                    pe.wait_ge(f_h_done, b * NB + j)
                e0 = slice(j * 128, (j + 1) * 128)
                pe.matmul(gu_bank[:, 0:T], w_gate[:, e0], xn2T[:, :], start=True, stop=True)
                pe.matmul(gu_bank[:, T:2 * T], w_up[:, e0], xn2T[:, :], start=True, stop=True).then_inc(gu_ready, 1)

            def down(b, j):
                pe.wait_ge(f_hc_done, b * NB + j + 1)
                for n in range(NQ):
                    last = pe.matmul(down_bank[:, n * 128:(n + 1) * 128], f_hc[:, j % RF, n * 128:(n + 1) * 128], w_down[:, j, :],
                                     start=j == 0 and n == 0, stop=j == NB - 1 and n == NQ - 1)
                last.then_inc(down_used, 1)

            def tick(t, par):
                for s in range(SLOTS):
                    for off, k in M1_SLOTS.get(s, []):
                        if on(t + off):
                            max_chunk(t + off, (par + off) % 2, k)
                    if on(t) and s < NC2:
                        exp_chunk(t, par, s)
                    for g in range(8):
                        if s == PV_SLOT[g] and on(t):
                            weigh_values(t, par, g)
                    for name, slot, off in MISC:
                        if slot == s and on(t + off):
                            misc_use(t, par, name, off)
                    for j in range(NB):
                        if s == FFN_SLOT[j] and on(t - 1):
                            gate_up(t - 1, j)
                    for j in range(NB):
                        if s == DOWN_SLOT[j] and on(t - 1):
                            down(t - 1, j)

            ticks(pe, tick)

        @block.vector
        def _(dve):
            for pads in (r_gin, r_gtop, r_ein, r_etop):
                nc.vector.memset(pads[:, :, :], PAD)

            def scale_constants():
                dve.wait_ge(w_first, 48)
                dve.wait_ge(w_rest, 48)
                nc.vector.tensor_scalar(bias_q[:, :], cols_sb[:, 0:2], SCALE, None, ALU.mult)
                nc.vector.tensor_tensor(bias_v[:, :], cols_sb[:, 4:5], cols_sb[:, 5:6], ALU.add).then_inc(scaled, 1)
                dve.wait_ge(gate_made, 1)
                nc.vector.tensor_scalar(gate[:, 2:3], gate[:, 1:2], ROUTED_SCALE / 2, None, ALU.mult).then_inc(gate_made, 1)
                nc.vector.tensor_scalar(bp_row[:, :], rows_sb[:, 0:C], gate[:, 0:1], None, ALU.mult).then_inc(gate_made, 1)

            def clear_stacks():
                for n in range(2):
                    for st in (q_stack, k_stack):
                        words = st[64:128, n].rearrange("p h o t -> p (h o t)").bitcast(mybir.dt.uint32)
                        nc.vector.memset(words, 0).then_inc(stack_cleared, 1)

            def stats(src, st, mv, step, done):
                for n in range(NQ):
                    nc.vector.bn_stats(st[:, n, :], src[:, n, :]).then_inc(step, 1)
                dve.wait_ge(step, NQ)
                dve.sem_clear(step)
                for n in range(NQ):
                    last = nc.vector.bn_aggr(mv[:, n, :], st[:, n, :])
                last.then_inc(done, 1)

            def normalise(src, mv, rs, dst, done):
                for n in range(NQ):
                    last = nc.vector.tensor_scalar(dst[:, n, :], src[:, n, :], mv[:, n, 0:1], rs[:, n:n + 1], ALU.subtract, ALU.mult)
                last.then_inc(done, 1)

            def take_max(b, k):
                kind, qt, h0, nh, keys = S1_CHUNKS[k]
                if k == 0:
                    ge(dve, misc_ready, misc_batch_number(b - 1, "shift_self") + 1 if not isinstance(b, int) or b > 0 else 0)
                dve.wait_ge(max_scores, b * NC1 + k + 1)
                nc.vector.tensor_reduce(row_max[:, kind, qt, h0:h0 + nh], max_bank[k % 2][:, :].rearrange("p (h k) -> p h k", h=nh),
                                        AX.X, ALU.max).then_inc(max_taken, 1)

            def shift(t, b, name, kind):
                dve.wait_ge(misc_ready, misc_number(t, name) + 1)
                ge(dve, shift_in[kind], b * 16)
                nc.vector.tensor_scalar(shiftT[:, kind, :], misc[0:H, 0:T], -1.0, None, ALU.mult).then_inc(misc_free, 1)

            def merge(t, b, i):
                dve.wait_ge(misc_ready, misc_number(t, f"y{i}") + 1)
                v = misc[:, :].rearrange("p (a v) -> p a v", v=VW)
                nc.vector.reciprocal(recip[:, :].unsqueeze(2), v[:, :, SUM_COL:SUM_COL + 1]).then_inc(y_step, 1)
                dve.wait_ge(y_step, 1)
                dve.sem_clear(y_step)
                half = slice((i % 2) * C // 2, (i % 2 + 1) * C // 2)
                r = recip[:, :].unsqueeze(2).broadcast_to([128, 16, D])
                if i < 2:
                    if i == 0:
                        ge(dve, misc_ready, misc_batch_number(b - 1, "yT") + 1 if not isinstance(b, int) or b > 0 else 0)
                    o = y[:, :, half].rearrange("p n (a d) -> p n a d", d=D)
                    nc.vector.tensor_tensor(o, v[:, :, 0:D].rearrange("p (n a) d -> p n a d", n=NQ),
                                            r.rearrange("p (n a) d -> p n a d", n=NQ), ALU.mult).then_inc(misc_free, 1)
                else:
                    nc.vector.tensor_tensor(y_tmp[:, :, :].rearrange("p n (a d) -> p (n a) d", d=D), v[:, :, 0:D], r,
                                            ALU.mult).then_inc(misc_free, 1)
                    dve.wait_ge(misc_free, misc_number(t, f"y{i}") + 1)
                    last = nc.vector.tensor_tensor(y[:, :, half], y[:, :, half], y_tmp[:, :, :], ALU.add)
                    if i == 3:
                        last.then_inc(y_done, 1)

            def route(b):
                count = [0]

                def step(ins):
                    count[0] += 1
                    ins.then_inc(route_step, 1)
                    dve.wait_ge(route_step, count[0])

                grouped = r_choice[:, :, :].rearrange("p n (g e) -> p (n g) e", g=GROUPS)
                step(nc.vector.tensor_scalar(r_score[:, :, :], r_tanh[:, :, :], 0.5, 0.5, ALU.mult, ALU.add))
                step(nc.vector.tensor_tensor(r_choice[:, :, :], r_score[:, :, :], rb_row[:, :].unsqueeze(1).broadcast_to([128, NQ, E]),
                                             ALU.add))
                nc.vector.tensor_tensor(r_pair[:, :, 0:3], grouped[:, :, 0:3], grouped[:, :, 1:4], ALU.add)
                nc.vector.tensor_tensor(r_pair[:, :, 3:5], grouped[:, :, 0:2], grouped[:, :, 2:4], ALU.add)
                step(nc.vector.tensor_tensor(r_pair[:, :, 5:6], grouped[:, :, 0:1], grouped[:, :, 3:4], ALU.add))
                step(nc.vector.tensor_reduce(r_gin[:, :, 0:GROUPS], r_pair[:, :, :].rearrange("p (n g) k -> p n g k", n=NQ), AX.X, ALU.max))
                for n in range(NQ):
                    step(nc.vector.max(r_g8[:, n, :], r_gin[:, n, :]))
                step(nc.vector.tensor_copy(r_gtop[:, :, 0:TOP_GROUPS], r_g8[:, :, 0:TOP_GROUPS]))
                for n in range(NQ):
                    step(nc.vector.match_replace(r_gout[:, n, :], r_gtop[:, n, :], r_gin[:, n, :], TAKEN))
                step(nc.vector.tensor_scalar(r_gsel[:, :, :], r_gout[:, :, 0:GROUPS], TAKEN, None, ALU.is_equal))
                step(nc.vector.tensor_scalar(r_gpen[:, :, :], r_gsel[:, :, :], -NEG_INF, NEG_INF, ALU.mult, ALU.add))
                per = E // GROUPS
                for n in range(NQ):
                    o = r_ein[:, n, 0:E].rearrange("p (g e) -> p g e", g=GROUPS)
                    ch = r_choice[:, n, :].rearrange("p (g e) -> p g e", g=GROUPS)
                    step(nc.vector.tensor_tensor(o, ch, r_gsel[:, n, :].unsqueeze(2).broadcast_to([128, GROUPS, per]), ALU.mult))
                    step(nc.vector.tensor_tensor(o, o, r_gpen[:, n, :].unsqueeze(2).broadcast_to([128, GROUPS, per]), ALU.add))
                for n in range(NQ):
                    step(nc.vector.max(r_e8[:, n, :], r_ein[:, n, :]))
                step(nc.vector.tensor_copy(r_etop[:, :, 0:TOP_EXPERTS], r_e8[:, :, 0:TOP_EXPERTS]))
                for n in range(NQ):
                    step(nc.vector.match_replace(r_eout[:, n, :], r_etop[:, n, :], r_ein[:, n, :], TAKEN))
                step(nc.vector.tensor_scalar(r_sel[:, :, :], r_eout[:, :, 0:E], TAKEN, None, ALU.is_equal))
                ge(dve, misc_ready, misc_batch_number(b - 1, "combT") + 1 if not isinstance(b, int) or b > 0 else 0)
                step(nc.vector.tensor_tensor(r_sel[:, :, :], r_sel[:, :, :], r_score[:, :, :], ALU.mult))
                step(nc.vector.tensor_reduce(r_sum[:, :], r_sel[:, :, :], AX.X, ALU.add))
                step(nc.vector.tensor_scalar(r_sum[:, :], r_sum[:, :], 1e-20, None, ALU.add))
                step(nc.vector.reciprocal(r_sum[:, :], r_sum[:, :]))
                dve.sem_clear(route_step)
                nc.vector.scalar_tensor_tensor(out=r_w[:, :, :], in0=r_sel[:, :, :], scalar=gate[:, 2:3],
                                               in1=r_sum[:, :].unsqueeze(2).broadcast_to([128, NQ, E]),
                                               op0=ALU.mult, op1=ALU.mult).then_inc(comb_done, 1)

            def expert_products(b, j):
                dve.wait_ge(f_tanh_done, b * NB + j + 1)
                nc.vector.scalar_tensor_tensor(out=f_gate[:, :], in0=f_tanh[:, :], scalar=1.0, in1=gu_bank[:, 0:T],
                                               op0=ALU.add, op1=ALU.mult).then_inc(f_gate_done, 1)
                dve.wait_ge(f_gate_done, b * NB + j + 1)
                if j >= RF:
                    dve.wait_ge(f_hc_done, b * NB + j + 1 - RF)
                nc.vector.tensor_tensor(f_h[:, j % RF, :], f_gate[:, :], gu_bank[:, T:2 * T], ALU.mult).then_inc(f_h_done, 1)

            def tick(t, par):
                p1 = 1 - par
                for s in range(SLOTS):
                    if s == 0 and on(t + 1):
                        b = t + 1
                        dve.wait_ge(x_loaded, b * 32 + 32)
                        stats(x_in[:, p1], stats1, mean1, ln1_step, stats_done)
                    if s == misc_slot("y3") and on(t - 1):
                        merge(t, t - 1, 3)
                    if s == 1 and on(t + 1):
                        b = t + 1
                        dve.wait_ge(rstd_done, b + 1)
                        ge(dve, misc_ready, misc_batch_number(b - 1, "xnT") + 1 if not isinstance(b, int) or b > 0 else 0)
                        normalise(x_in[:, p1], mean1, rstd1, xn, xn_done)
                        if isinstance(t, int) and t == FIRST_TICK:
                            scale_constants()
                            clear_stacks()
                    for off, k in M1_SLOTS.get(s, []):
                        if on(t + off):
                            take_max(t + off, k)
                    if s == misc_slot("wp") and on(t - 1):
                        b = t - 1
                        dve.wait_ge(misc_ready, misc_number(t, "wp") + 1)
                        dve.wait_ge(res_done, b + 1)
                        nc.vector.scalar_tensor_tensor(out=x1[:, :, :], in0=misc[:, 0:T].rearrange("p (n c) -> p n c", n=NQ),
                                                       scalar=gate[:, 0:1], in1=x_res[:, 1 - par], op0=ALU.mult, op1=ALU.add)\
                            .then_inc(misc_free, 1)
                        dve.wait_ge(misc_free, misc_number(t, "wp") + 1)
                        stats(x1, stats2, mean2, ln2_step, stats2_done)
                    if s == misc_slot("xn2T") - 1 and on(t - 1):
                        b = t - 1
                        dve.wait_ge(rstd2_done, b + 1)
                        ge(dve, misc_ready, misc_batch_number(b - 1, "xn2T") + 1 if not isinstance(b, int) or b > 0 else 0)
                        normalise(x1, mean2, rstd2, xn2, xn2_done)
                    if s == misc_slot("route") + 1 and on(t - 1):
                        dve.wait_ge(misc_free, misc_number(t, "route") + 1)
                        route(t - 1)
                    if s == misc_slot("shift_cross") and on(t):
                        shift(t, t, "shift_cross", CROSS)
                    if s == misc_slot("shift_self") and on(t + 1):
                        shift(t, t + 1, "shift_self", SELF)
                    for i in range(3):
                        if s == misc_slot(f"y{i}") and on(t):
                            merge(t, t, i)
                    for j in range(NB):
                        if s == FFN_SLOT[j] and on(t - 1):
                            expert_products(t - 1, j)
                    if s == SLOTS - 1 and on(t - 1):
                        b = t - 1
                        dve.wait_ge(down_used, b * NB + NB)
                        dve.wait_ge(stored, b * 16 + 16)
                        nc.vector.tensor_tensor(y_out[:, :, :], down_bank[:, 0:T].rearrange("p (n c) -> p n c", n=NQ), x1[:, :, :],
                                                ALU.add).then_inc(out_done, 1)

            ticks(dve, tick)


_P = "L0_xattn_"
_F = "L0_ffn_"


def kernel(**inputs):
    import numpy as np
    import concourse.bacc as bacc
    from concourse.bass_utils import run_bass_kernel_spmd

    a = {k: np.asarray(v) for k, v in inputs.items()}
    p = lambda n: a[_P + n]
    ins = {
        "x": a["x"], "ctxT": a["ctx_512"].transpose(2, 0, 1),
        "w_model": np.concatenate([p("Wq"), p("Wcq"), p("Wk"), p("Wv"), p("Wp"), a[_F + "router_weight"].T], axis=1),
        "w_ctx": np.concatenate([p("Wck"), p("Wcv")], axis=1),
        "cols": np.stack([p("bq"), p("bcq"), p("bk"), p("bck"), p("bv"), p("bcv")], axis=1),
        "rows": np.concatenate([p("bp"), a[_F + "router_bias"], a["g_xattn"], a["g_ffn"]]),
        "w_pairs": np.stack([a[_F + n].transpose(2, 0, 1).reshape(C, E * I) for n in ("w_gate", "w_up")], axis=1),
        "w_down": a[_F + "w_down"].transpose(0, 2, 1).reshape(NB, 128, C).transpose(1, 0, 2),
    }
    nc = bacc.Bacc("TRN2", target_bir_lowering=False, num_devices=1)
    arrays, args = {}, []
    for name, v in ins.items():
        v = np.ascontiguousarray(v)
        arrays["in_" + name] = v
        args.append(nc.dram_tensor("in_" + name, v.shape, mybir.dt.from_np(v.dtype), kind="ExternalInput").ap())
    out = nc.dram_tensor("out", (B, T, C), FP32, kind="ExternalOutput").ap()
    build(nc, *args, out)
    r = run_bass_kernel_spmd(nc, [arrays], core_ids=[0])
    return r.results[0]["out"]
```

```python
import concourse.bass as bass
from concourse import mybir
from contextlib import ExitStack

FP32 = mybir.dt.float32
BF16 = mybir.dt.bfloat16
ALU = mybir.AluOpType
ACT = mybir.ActivationFunctionType
AX = mybir.AxisListType

B, T, C, CC, H, E, I = 8, 256, 128, 64, 16, 16, 64
D = C // H
NQ = T // 128
SCALE = D ** -0.5
EPS = 1e-5
NEG_INF = -1e9
MASKED = -1e30
PAD = -3e38
TAKEN = -2e38
TOP_GROUPS, TOP_EXPERTS, GROUPS = 2, 4, 4
ROUTED_SCALE = 2.5

PARTS = 3
STACK = PARTS * PARTS * D
SHIFT_ROW = STACK
VW = 32
SUM_COL = D

SELF, CROSS = 0, 1
NB = E * I // 128

S2_CHUNKS = []
S2_GROUP = []
for g in range(H // 4):
    S2_CHUNKS += [(CROSS, kt, 4 * g + hp, 2, 0) for kt in range(NQ) for hp in (0, 2)]
    S2_GROUP += [g] * 4
for g in range(H // 4):
    S2_CHUNKS += [(SELF, 0, 4 * g, 2, 0), (SELF, 0, 4 * g + 2, 2, 0), (SELF, 1, 4 * g, 4, 128)]
    S2_GROUP += [H // 4 + g] * 3
NC2 = len(S2_CHUNKS)
CROSS_C2 = 4 * (H // 4)
SELF_C2 = NC2 - CROSS_C2
LAST_CHUNK = [max(c for c in range(NC2) if S2_GROUP[c] == g) for g in range(8)]
NP = 7
assert NC2 % NP == 0 and NC2 % 2 == 0

S1_CHUNKS = [(CROSS, qt, 2 * g, 2, 256) for qt in range(NQ) for g in range(8)]
CROSS_C1 = len(S1_CHUNKS)
S1_CHUNKS += [(SELF, 0, 4 * g, 4, 128) for g in range(4)] + [(SELF, 1, 2 * g, 2, 256) for g in range(8)]
NC1 = len(S1_CHUNKS)

ORDERS = {
    'pe': '''
        max:16 xnT max:17 exp:0 y3 max:18 max:19 exp:1 qproj exp:2 yT max:20 exp:3 kproj wp max:21 pv:0 exp:4 max:22 max:23
        vproj max:24 exp:5 exp:6 max:25 exp:7 exp:8 xn2T max:26 exp:9 max:27 pv:1 exp:10 exp:11 logits gate_up:0 shift_self
        exp:12 exp:13 y0 gate_up:1 pv:2 exp:14 max:0 max:1 exp:15 max:2 gate_up:2 max:3 exp:16 max:4 exp:17 max:5 pv:3 max:6
        combT gate_up:3 max:7 max:8 exp:18 exp:19 max:9 max:10 exp:20 y1 gate_up:4 gate_up:5 max:11 exp:21 max:12 pv:4 down:0
        max:13 gate_up:6 down:1 down:2 exp:22 exp:23 down:3 down:4 exp:24 max:14 exp:25 pv:5 max:15 exp:26 gate_up:7 down:5
        exp:27 shift_cross pv:6 down:6 y2 pv:7 down:7''',
    'act': '''
        xnT exp:0 exp:1 qproj yT exp:2 exp:3 kproj k_part0 vproj exp:4 exp:5 exp:6 exp:7 exp:8 exp:9 xn2T logits exp:10 tanh:0
        exp:11 pv_copy:0 exp:12 exp:13 tanh:1 exp:14 exp:15 tanh:2 combT exp:16 tanh:3 exp:17 exp:18 exp:19 pv_copy:1 exp:20
        tanh:4 tanh:5 tanh:6 exp:21 exp:22 exp:23 exp:24 exp:25 pv_copy:2 tanh:7 exp:26 exp:27 pv_copy:3''',
    'dve': '''
        max:16 max:17 y:3 max:18 max:19 queries:0 max:20 queries:1 queries:2 queries:3 x1 max:21 stats2 max:22 max:23 max:24 xn2
        max:25 max:26 max:27 route:0 route:1 route:2 swish:0 shift_self route:3 route:4 times_up:0 route:5 route:6 swish:1
        route:7 times_up:1 max:0 max:1 route:8 max:2 y:0 route:9 route:10 max:3 route:11 swish:2 route:12 times_up:2 route:13
        route:14 route:15 route:16 max:4 route:17 max:5 max:6 swish:3 max:7 times_up:3 max:8 stats1 swish:4 max:9 times_up:4
        max:10 max:11 swish:5 times_up:5 max:12 swish:6 max:13 y:1 times_up:6 max:14 max:15 swish:7 times_up:7 shift_cross xn1
        y:2 out''',
    'pool': '''
        keys:1 keys:2 rstd2 keys:3 residual mask:16 mask:17 mask:18 weight:0 weight:1 weight:2 weight:3 mask:19 weight:4 mask:20
        mask:21 weight:5 mask:22 mask:23 mask:24 rstd1 mask:25 weight:6 mask:26 mask:27 weight:7''',
    'sp': '''
        load shift_rows q_part:0 q_part:1 q_part:2 k_part:0 q_stack:1 q_stack:0 k_part:1 k_part:2 k_stack:1 k_stack:0 shift_self comb_out comb_in
        shift_cross out''',
}
MISC_BATCH = dict(xnT=1, qproj=1, kproj=1, vproj=1, shift_cross=1, shift_self=0, y0=0, y1=0, y2=0, y3=-1, yT=-1, wp=-1,
                  xn2T=-1, logits=-1, combT=-1)
MISC = [(name, MISC_BATCH[name]) for name in ORDERS["pe"].split() if name in MISC_BATCH]
NMISC = len(MISC)
ROUTE_STEPS = 18
FIRST_TICK, LOOP_LO, LOOP_HI, LAST_TICK = -1, 1, 7, B


def on(b):
    return not isinstance(b, int) or 0 <= b < B


def misc_number(t, name):
    at = [m[0] for m in MISC].index(name)
    full = lambda u: [on(u + m[1]) for m in MISC]
    if isinstance(t, int):
        return sum(sum(full(u)) for u in range(FIRST_TICK, t)) + sum(full(t)[:at])
    before = sum(sum(full(u)) for u in range(FIRST_TICK, LOOP_LO))
    return (t - LOOP_LO) * NMISC + (before + at)


def misc_batch_number(b, name):
    off = MISC_BATCH[name]
    return misc_number(b - off, name)


def build(nc, x, ctxT, w_model, w_ctx, cols, rows, w_pairs, w_down_in, out):
    stack = ExitStack()
    with stack:
        def sb(name, shape, dt=FP32):
            return stack.enter_context(nc.sbuf_tensor(name, shape, dt))

        def sem(name):
            return stack.enter_context(nc.semaphore(name))

        w_model_sb = sb("w_model_sb", [C, 5 * C + E])
        w_q, w_cq, w_k, w_v, w_p = (w_model_sb[:, n * C:(n + 1) * C] for n in range(5))
        w_router = w_model_sb[:, 5 * C:5 * C + E]
        w_ctx_sb = sb("w_ctx_sb", [CC, 2 * C])
        w_ck, w_cv = w_ctx_sb[:, 0:C], w_ctx_sb[:, C:2 * C]
        w_pairs_sb = sb("w_pairs_sb", [C, 2, E * I])
        w_gate, w_up = w_pairs_sb[:, 0, :], w_pairs_sb[:, 1, :]
        w_down = sb("w_down", [128, NB, C])
        cols_sb = sb("cols_sb", [C, 6])
        bias_q = sb("bias_q", [C, 2])
        bias_v = sb("bias_v", [C, 1])
        rows_sb = sb("rows_sb", [128, C + E + 2])
        rb_row, gates = rows_sb[:, C:C + E], rows_sb[:, C + E:C + E + 2]
        bp_row = sb("bp_row", [128, C])
        gate = sb("gate", [128, 3])
        minus_half = sb("minus_half", [128, NQ])
        ident = sb("ident", [128, 128])
        ident_b = sb("ident_b", [128, 128], BF16)
        causal = sb("causal", [128, 4, 128], BF16)
        zero_row = sb("zero_row", [2 * H, T], BF16)
        ones_row = sb("ones_row", [2 * H, T], BF16)

        x_in = sb("x_in", [128, 2, NQ, C])
        ctx_in = sb("ctx_in", [CC, 2, T])
        stats1, mean1, rstd1 = sb("stats1", [128, NQ, 6]), sb("mean1", [128, NQ, 2]), sb("rstd1", [128, NQ])
        xn = sb("xn", [128, NQ, C])
        xnT = sb("xnT", [C, T])
        proj = sb("proj", [C, 2, 2 * T])
        rest = sb("rest", [C, 2, 2 * T])
        part = sb("part", [C, 2, PARTS, 2 * T], BF16)
        q_stack = sb("q_stack", [128, 2, 2, H, T], BF16)
        k_stack = sb("k_stack", [128, 2, 2, H, T], BF16)
        v_ext = sb("v_ext", [128, 2, 2, NQ, H, VW])
        row_max = sb("row_max", [128, 2, NQ, H])
        shiftT = sb("shiftT", [H, 2, T], BF16)
        probs = sb("probs", [128, NP, 512])
        y_raw = sb("y_raw", [128, 2, 512])
        recip = sb("recip", [128, 16])
        y_tmp = sb("y_tmp", [128, NQ, C // 2])
        y = sb("y", [128, NQ, C])
        yT = sb("yT", [C, T])
        x_res = sb("x_res", [128, 2, NQ, C])
        x1 = sb("x1", [128, NQ, C])
        stats2, mean2, rstd2 = sb("stats2", [128, NQ, 6]), sb("mean2", [128, NQ, 2]), sb("rstd2", [128, NQ])
        xn2 = sb("xn2", [128, NQ, C])
        xn2T = sb("xn2T", [C, T])
        r_tanh, r_score, r_choice = (sb(n, [128, NQ, E]) for n in ("r_tanh", "r_score", "r_choice"))
        r_pair = sb("r_pair", [128, NQ * GROUPS, 6])
        r_gin, r_gout = sb("r_gin", [128, NQ, 10]), sb("r_gout", [128, NQ, 10])
        r_g8, r_gtop = sb("r_g8", [128, NQ, 8]), sb("r_gtop", [128, NQ, 8])
        r_gsel, r_gpen = sb("r_gsel", [128, NQ, GROUPS]), sb("r_gpen", [128, NQ, GROUPS])
        r_ein, r_eout = sb("r_ein", [128, NQ, 20]), sb("r_eout", [128, NQ, 20])
        r_e8, r_etop = sb("r_e8", [128, NQ, 8]), sb("r_etop", [128, NQ, 8])
        r_sel, r_w = sb("r_sel", [128, NQ, E]), sb("r_w", [128, NQ, E])
        r_sum = sb("r_sum", [128, NQ])
        combT = sb("combT", [E, T])
        comb = sb("comb", [128, NB, T])
        f_tanh, f_gate = sb("f_tanh", [128, T]), sb("f_gate", [128, T])
        f_h, f_hc = sb("f_h", [128, NB, T]), sb("f_hc", [128, NB, T])
        y_out = sb("y_out", [128, NQ, C])

        q_scr = nc.dram_tensor("q_scr", (2, 2, PARTS, D, H, T), BF16).ap()
        k_scr = nc.dram_tensor("k_scr", (2, 2, PARTS, D, H, T), BF16).ap()
        c_scr = nc.dram_tensor("c_scr", (E, T), FP32).ap()

        bank = [stack.enter_context(nc.psum_tensor(f"bank{n}", [128, 512], FP32)) for n in range(8)]
        max_bank, exp_bank, pv_bank, down_bank, gu_bank, misc = bank[0:2], bank[2:4], bank[4], bank[5], bank[6], bank[7]

        w_first = sem("w_first")
        w_rows = sem("w_rows")
        w_experts = sem("w_experts")
        ones_in = sem("ones_in")
        v_cleared = sem("v_cleared")
        stack_cleared = sem("stack_cleared")
        const_made = sem("const_made")
        const_step = sem("const_step")
        scaled = sem("scaled")
        gate_made = sem("gate_made")
        x_loaded = sem("x_loaded")
        stats_done = sem("stats_done")
        rstd_done = sem("rstd_done")
        rstd_step = sem("rstd_step")
        xn_done = sem("xn_done")
        ln1_step = sem("ln1_step")
        q_rest = sem("q_rest")
        split_step = sem("split_step")
        q_split, k_split = sem("q_split"), sem("k_split")
        q_stored, k_stored = sem("q_stored"), sem("k_stored")
        shift_cleared = sem("shift_cleared")
        stack_in = [sem("stack_in_self"), sem("stack_in_cross")]
        res_done = sem("res_done")
        max_scores = sem("max_scores")
        max_taken = sem("max_taken")
        shift_in = [sem("shift_in_self"), sem("shift_in_cross")]
        exp_scores = sem("exp_scores")
        exp_done = sem("exp_done")
        mask_done = sem("mask_done")
        pv_done = sem("pv_done")
        pv_copied = sem("pv_copied")
        y_step = sem("y_step")
        y_done = sem("y_done")
        misc_ready = sem("misc_ready")
        misc_free = sem("misc_free")
        ln2_step = sem("ln2_step")
        stats2_done = sem("stats2_done")
        rstd2_done = sem("rstd2_done")
        rstd2_step = sem("rstd2_step")
        xn2_done = sem("xn2_done")
        route_step = sem("route_step")
        comb_done = sem("comb_done")
        comb_stored = sem("comb_stored")
        comb_in = sem("comb_in")
        gu_ready = sem("gu_ready")
        f_tanh_done = sem("f_tanh_done")
        f_gate_done = sem("f_gate_done")
        f_h_done = sem("f_h_done")
        f_hc_done = sem("f_hc_done")
        down_used = sem("down_used")
        out_done = sem("out_done")
        stored = sem("stored")
        pool_carrier, sp_carrier = sem("pool_carrier"), sem("sp_carrier")

        block = stack.enter_context(nc.Block())

        def ge(eng, s, v):
            if not isinstance(v, int) or v > 0:
                eng.wait_ge(s, v)

        def ticks(eng, tick):
            for t in range(FIRST_TICK, LOOP_LO):
                tick(t, t % 2)
            with eng.Fori(LOOP_LO, LOOP_HI, 2) as t:
                tick(t, LOOP_LO % 2)
                tick(t + 1, (LOOP_LO + 1) % 2)
            for t in range(LOOP_HI, LAST_TICK + 1):
                tick(t, t % 2)

        def steps(engine):
            for word in ORDERS[engine].split():
                what, _, n = word.partition(":")
                yield what, int(n or 0)

        @block.sync
        def _(sp):
            def load_x(b, par):
                sp.dma_start(x_in[:, par], x[b].rearrange("(n p) c -> p n c", p=128)).then_inc(x_loaded, 16)
                sp.dma_start(ctx_in[:, par], ctxT[:, b]).then_inc(x_loaded, 16)

            load_x(0, 0)
            sp.dma_start(w_model_sb[:, :], w_model).then_inc(w_first, 16)
            sp.dma_start(w_ctx_sb[:, :], w_ctx).then_inc(w_first, 16)
            sp.dma_start(cols_sb[:, :], cols).then_inc(w_first, 16)
            sp.dma_start(rows_sb[:, :], rows.partition_broadcast(128)).then_inc(w_rows, 16)
            sp.dma_start(w_pairs_sb[:, :, :], w_pairs).then_inc(w_experts, 16)
            sp.dma_start(w_down[:, :, :], w_down_in).then_inc(w_experts, 16)

            def tick(t, par):
                b, p1 = t + 1, 1 - par
                for what, n in steps("sp"):
                    if what == "load" and on(t + 2):
                        ge(sp, x_loaded, (t + 2) * 32)
                        sp.sem_inc(sp_carrier, 1)
                        ge(sp, res_done, t + 1)
                        sp.sem_inc(sp_carrier, 1)
                        if on(t):
                            ge(sp, misc_free, misc_number(t - 1, "vproj") + 1)
                        load_x(t + 2 if isinstance(t, int) else (t + 2) % B, par)
                    elif what == "q_part" and on(b):
                        ge(sp, q_split, b * PARTS + n + 1)
                        sp.dma_start(q_scr[p1, :, n].rearrange("k d h x -> (d h) k x"), part[:, 0, n, :].rearrange("c (k x) -> c k x", k=2)).then_inc(q_stored, 16)
                    elif what == "k_part" and on(b):
                        ge(sp, k_split, b * PARTS + n + 1)
                        sp.dma_start(k_scr[p1, :, n].rearrange("k d h x -> (d h) k x"), part[:, 1, n, :].rearrange("c (k x) -> c k x", k=2)).then_inc(k_stored, 16)
                    elif what == "shift_rows" and on(b):
                        ge(sp, pv_done, (b - 1) * 8)
                        sp.sem_inc(sp_carrier, 1)
                        if isinstance(t, int) and b < 2:
                            sp.wait_ge(stack_cleared, (3, 7)[b])
                            sp.dma_start(k_stack[SHIFT_ROW:SHIFT_ROW + 1, p1], ones_row[:, :]).then_inc(ones_in, 16)
                        sp.dma_start(q_stack[SHIFT_ROW:SHIFT_ROW + 1, p1], zero_row[:, :]).then_inc(shift_cleared, 16)
                    elif what == "q_stack" and on(b):
                        ge(sp, q_stored, b * 48 + 48)
                        for i in range(PARTS):
                            src = q_scr[p1, n, i].rearrange("d h x -> d (h x)").unsqueeze(0).broadcast_to([PARTS, D, H * T])
                            sp.dma_start(q_stack[i * PARTS * D:(i + 1) * PARTS * D, p1, n], src).then_inc(stack_in[n], 16)
                    elif what == "k_stack" and on(b):
                        ge(sp, k_stored, b * 48 + 48)
                        src = k_scr[p1, n].rearrange("j d h x -> (j d) (h x)").unsqueeze(0).broadcast_to([PARTS, PARTS * D, H * T])
                        sp.dma_start(k_stack[0:STACK, p1, n], src).then_inc(stack_in[n], 16)
                    elif what == "shift_self" and on(t):
                        ge(sp, misc_free, misc_number(t, "shift_self") + 1)
                        sp.dma_start(q_stack[SHIFT_ROW:SHIFT_ROW + 1, par, SELF], shiftT[:, SELF, :]).then_inc(shift_in[SELF], 16)
                    elif what == "shift_cross" and on(b):
                        ge(sp, misc_free, misc_number(t, "shift_cross") + 1)
                        sp.dma_start(q_stack[SHIFT_ROW:SHIFT_ROW + 1, p1, CROSS], shiftT[:, CROSS, :]).then_inc(shift_in[CROSS], 16)
                    elif what == "comb_out" and on(t - 1):
                        ge(sp, misc_free, misc_number(t, "combT") + 1)
                        sp.dma_start(c_scr, combT[:, :]).then_inc(comb_stored, 16)
                    elif what == "comb_in" and on(t - 1):
                        sp.wait_ge(comb_stored, t * 16)
                        for e2 in range(2):
                            src = c_scr.rearrange("(j e) t -> e j t", e=2)[e2].partition_broadcast(I)
                            sp.dma_start(comb[e2 * I:(e2 + 1) * I, :, :], src).then_inc(comb_in, 16)
                    elif what == "out" and on(t - 1):
                        ge(sp, out_done, t)
                        sp.dma_start(out[t - 1].rearrange("(n p) c -> p n c", p=128), y_out[:, :, :]).then_inc(stored, 16)

            sp.sem_inc(stored, 16)
            ticks(sp, tick)
            sp.wait_ge(x_loaded, 32 * (LOOP_HI - 1 + 3))
            sp.wait_ge(stored, 16 * B + 16)
            sp.wait_ge(q_stored, 48 * B)
            sp.wait_ge(k_stored, 48 * B)
            sp.wait_ge(comb_stored, 16 * B)

        @block.gpsimd
        def _(pool):
            nc.gpsimd.memset(ident[:, :], 0.0).then_inc(const_step, 1)
            nc.gpsimd.memset(minus_half[:, :], -0.5).then_inc(const_step, 1)
            nc.gpsimd.memset(causal[:, :, :], 0.0).then_inc(const_step, 1)
            nc.gpsimd.memset(ident_b[:, :], 0.0).then_inc(const_step, 1)
            nc.gpsimd.memset(zero_row[:, :], 0.0).then_inc(const_step, 1)
            nc.gpsimd.memset(ones_row[:, :], 1.0).then_inc(const_step, 1)
            pool.wait_ge(const_step, 6)
            nc.gpsimd.affine_select(out=ident[:, :], in_=ident[:, :], compare_op=ALU.not_equal, fill=1.0, base=0,
                                    pattern=[[-1, 128]], channel_multiplier=1).then_inc(const_made, 1)
            nc.gpsimd.affine_select(out=ident_b[:, :], in_=ident_b[:, :], compare_op=ALU.not_equal, fill=1.0, base=0,
                                    pattern=[[-1, 128]], channel_multiplier=1).then_inc(const_made, 1)
            nc.gpsimd.affine_select(out=causal[:, :, :], in_=causal[:, :, :], compare_op=ALU.is_ge, fill=MASKED, base=0,
                                    pattern=[[0, 4], [-1, 128]], channel_multiplier=1).then_inc(const_made, 1)

            def clear_values():
                v = v_ext[:, :, :, :, :, :].rearrange("p a k n h v -> p (a k n h) v")
                nc.gpsimd.memset(v, 0.0).then_inc(const_step, 1)
                pool.wait_ge(const_step, 7)
                nc.gpsimd.memset(v[:, :, SUM_COL:SUM_COL + 1], 1.0).then_inc(v_cleared, 1)

            def rstd(mv, rs, ready, b, step, done):
                pool.wait_ge(ready, b + 1)
                pool.sem_inc(pool_carrier, 1)
                nc.gpsimd.tensor_scalar(rs[:, :], mv[:, :, 1], EPS, None, ALU.add).then_inc(step, 1)
                pool.wait_ge(step, 1)
                pool.sem_clear(step)
                nc.gpsimd.tensor_tensor(rs[:, :], rs[:, :], minus_half[:, :], ALU.pow).then_inc(done, 1)

            def split_keys(t, b, n):
                src, rem, prt = proj[:, 1, :], rest[:, 1, :], part[:, 1]
                if n == 1:
                    pool.wait_ge(k_split, b * PARTS + 1)
                    nc.gpsimd.tensor_tensor(rem, src, prt[:, 0, :], ALU.subtract).then_inc(split_step, 1)
                elif n == 2:
                    pool.wait_ge(split_step, 1)
                    pool.sem_clear(split_step)
                    nc.gpsimd.tensor_scalar(prt[:, 1, :], rem, 1.0, None, ALU.mult).then_inc(k_split, 1)
                else:
                    pool.wait_ge(k_split, b * PARTS + 2)
                    nc.gpsimd.tensor_tensor(prt[:, 2, :], rem, prt[:, 1, :], ALU.subtract).then_inc(k_split, 1)

            def mask(b, s):
                _, kt, h0, nh, q0 = S2_CHUNKS[s]
                pool.wait_ge(exp_done, b * NC2 + s + 1)
                pool.sem_inc(pool_carrier, 1)
                p = probs[:, s % NP, :].rearrange("p (h q) -> p h q", h=nh)[:, :, 0:128]
                nc.gpsimd.affine_select(out=p, in_=p, compare_op=ALU.is_ge, fill=0.0, base=0,
                                        pattern=[[0, nh], [1, 128]], channel_multiplier=-1).then_inc(mask_done, 1)

            def combine(b, j):
                pool.wait_ge(f_h_done, b * NB + j + 1)
                if j == 0:
                    pool.wait_ge(comb_in, b * 32 + 32)
                nc.gpsimd.tensor_tensor(f_hc[:, j, :], f_h[:, j, :], comb[:, j, :], ALU.mult).then_inc(f_hc_done, 1)

            def tick(t, par):
                for what, n in steps("pool"):
                    if what == "mask" and on(t):
                        mask(t, n)
                    elif what == "keys" and on(t + 1):
                        split_keys(t, t + 1, n)
                    elif what == "rstd2" and on(t - 1):
                        rstd(mean2, rstd2, stats2_done, t - 1, rstd2_step, rstd2_done)
                    elif what == "rstd1" and on(t + 2):
                        rstd(mean1, rstd1, stats_done, t + 2, rstd_step, rstd_done)
                    elif what == "residual" and on(t + 1):
                        b, p1 = t + 1, 1 - par
                        pool.wait_ge(x_loaded, b * 32 + 32)
                        if isinstance(t, int) and t == FIRST_TICK:
                            pool.wait_ge(gate_made, 3)
                        if on(b - 2):
                            ge(pool, misc_free, misc_number(t, "wp") + 1)
                        nc.gpsimd.tensor_tensor(x_res[:, p1], x_in[:, p1],
                                                bp_row[:, :].unsqueeze(1).broadcast_to([128, NQ, C]), ALU.add).then_inc(res_done, 1)
                    elif what == "weight" and on(t - 1):
                        combine(t - 1, n)

            rstd(mean1, rstd1, stats_done, 0, rstd_step, rstd_done)
            clear_values()
            ticks(pool, tick)

        @block.scalar
        def _(act):
            act.wait_ge(const_step, 2)
            words = k_stack[64:128, 0].rearrange("p k h t -> p (k h t)").bitcast(mybir.dt.float32)
            nc.scalar.activation(words, minus_half[64:128, 0:1].broadcast_to([64, words.shape[1]]), ACT.Copy, scale=0.0).then_inc(stack_cleared, 1)
            act.wait_ge(w_rows, 16)
            nc.scalar.activation(gate[:, 0:2], gates, ACT.Tanh).then_inc(gate_made, 1)
            def take(t, name):
                act.wait_ge(misc_ready, misc_number(t, name) + 1)

            def evacuate_pv(b, i):
                act.wait_ge(pv_done, b * 8 + 2 * i + 2)
                prev = misc_batch_number(b, f"y{i - 2}") if i >= 2 else misc_batch_number(b - 1, f"y{i + 2}")
                if i >= 2 or on(b - 1):
                    ge(act, misc_ready, prev + 1)
                nc.scalar.activation(y_raw[:, i % 2, :], pv_bank[:, :], ACT.Copy).then_inc(pv_copied, 1)

            def tick(t, par):
                p1 = 1 - par
                for what, n in steps("act"):
                    if what == "exp" and on(t):
                        act.wait_ge(exp_scores, t * NC2 + n + 1)
                        old = n - NP
                        if old >= 0:
                            act.wait_ge(pv_done, t * 8 + S2_GROUP[old] + 1)
                        else:
                            ge(act, pv_done, (t - 1) * 8 + S2_GROUP[old + NC2] + 1 if not isinstance(t, int) or t > 0 else 0)
                        nc.scalar.activation(probs[:, n % NP, :], exp_bank[n % 2][:, :], ACT.Exp).then_inc(exp_done, 1)
                    elif what == "tanh" and on(t - 1):
                        b = t - 1
                        act.wait_ge(gu_ready, b * NB + n + 1)
                        if n:
                            act.wait_ge(f_gate_done, b * NB + n)
                        nc.scalar.activation(f_tanh[:, :], gu_bank[:, 0:T], ACT.Tanh, scale=0.5).then_inc(f_tanh_done, 1)
                    elif what == "xnT" and on(t + 1):
                        take(t, what)
                        nc.scalar.activation(xnT[:, :], misc[:, 0:T], ACT.Copy).then_inc(misc_free, 1)
                    elif what == "yT" and on(t - 1):
                        take(t, what)
                        nc.scalar.activation(yT[:, :], misc[:, 0:T], ACT.Identity, bias=bias_v[:, :]).then_inc(misc_free, 1)
                    elif what == "qproj" and on(t + 1):
                        take(t, what)
                        if isinstance(t, int) and t == FIRST_TICK:
                            act.wait_ge(scaled, 1)
                        ge(act, q_split, (t + 1) * PARTS)
                        nc.scalar.activation(proj[:, 0, 0:T], misc[:, 0:T], ACT.Identity, bias=bias_q[:, 0:1], scale=SCALE)
                        nc.scalar.activation(proj[:, 0, T:2 * T], misc[:, T:2 * T], ACT.Identity, bias=bias_q[:, 1:2],
                                             scale=SCALE).then_inc(misc_free, 1)
                    elif what == "kproj" and on(t + 1):
                        take(t, what)
                        ge(act, k_split, (t + 1) * PARTS)
                        nc.scalar.activation(proj[:, 1, 0:T], misc[:, 0:T], ACT.Identity, bias=cols_sb[:, 2:3])
                        nc.scalar.activation(proj[:, 1, T:2 * T], misc[:, T:2 * T], ACT.Identity,
                                             bias=cols_sb[:, 3:4]).then_inc(misc_free, 1)
                    elif what == "k_part0" and on(t + 1):
                        act.wait_ge(misc_free, misc_number(t, "kproj") + 1)
                        ge(act, k_stored, (t + 1) * 48)
                        nc.scalar.activation(part[:, 1, 0, :], proj[:, 1, :], ACT.Copy).then_inc(k_split, 1)
                    elif what == "vproj" and on(t + 1):
                        take(t, what)
                        act.wait_ge(v_cleared, 1)
                        for kind in (SELF, CROSS):
                            last = nc.scalar.activation(
                                v_ext[:, p1, kind, :, :, 0:D],
                                misc[:, kind * T:(kind + 1) * T].rearrange("p (n h d) -> p n h d", n=NQ, d=D), ACT.Copy)
                        last.then_inc(misc_free, 1)
                    elif what == "xn2T" and on(t - 1):
                        take(t, what)
                        nc.scalar.activation(xn2T[:, :], misc[:, 0:T], ACT.Copy).then_inc(misc_free, 1)
                    elif what == "logits" and on(t - 1):
                        take(t, what)
                        nc.scalar.activation(r_tanh[:, :, :], misc[:, 0:NQ * E].rearrange("p (n e) -> p n e", n=NQ), ACT.Tanh,
                                             scale=0.5).then_inc(misc_free, 1)
                    elif what == "combT" and on(t - 1):
                        take(t, what)
                        nc.scalar.activation(combT[:, :], misc[0:E, 0:T], ACT.Copy).then_inc(misc_free, 1)
                    elif what == "pv_copy" and on(t):
                        evacuate_pv(t, n)

            ticks(act, tick)

        @block.tensor
        def _(pe):
            pe.wait_ge(w_first, 48)
            pe.wait_ge(const_made, 3)

            def max_chunk(b, par, k):
                kind, qt, h0, nh, keys = S1_CHUNKS[k]
                if k == 0:
                    pe.wait_ge(shift_cleared, b * 16 + 16)
                if k in (0, CROSS_C1):
                    pe.wait_ge(stack_in[kind], b * 64 + 64)
                if k == 0:
                    if isinstance(b, int) and b < 2:
                        pe.wait_ge(ones_in, 16 * b + 16)
                ge(pe, max_taken, b * NC1 + k - 1)
                ps = max_bank[k % 2][:, :].rearrange("p (h k) -> p h k", h=nh)
                if kind == SELF:
                    pe.matmul(ps[:, :, keys - 128:keys], ident_b[:, :], causal[:, 0:nh, :], start=True, stop=False)
                for n in range(nh):
                    h = h0 + n
                    q = q_stack[:, par, kind, h, qt * 128:(qt + 1) * 128]
                    if kind == SELF:
                        for kt in range(keys // 128):
                            last = pe.matmul(ps[:, n, kt * 128:(kt + 1) * 128], q, k_stack[:, par, kind, h, kt * 128:(kt + 1) * 128],
                                             start=False, stop=n == nh - 1 and kt == keys // 128 - 1)
                    else:
                        last = pe.matmul(ps[:, n, :], q, k_stack[:, par, kind, h, :], start=n == 0, stop=n == nh - 1)
                last.then_inc(max_scores, 1)

            def exp_chunk(t, par, s):
                kind, kt, h0, nh, q0 = S2_CHUNKS[s]
                if s in (0, CROSS_C2):
                    pe.wait_ge(shift_in[kind], t * 16 + 16)
                ge(pe, exp_done, t * NC2 + s - 1)
                ps = exp_bank[s % 2][:, :].rearrange("p (h q) -> p h q", h=nh)
                for n in range(nh):
                    h = h0 + n
                    last = pe.matmul(ps[:, n, :], k_stack[:, par, kind, h, kt * 128:(kt + 1) * 128],
                                     q_stack[:, par, kind, h, q0:T], start=n == 0, stop=n == nh - 1)
                last.then_inc(exp_scores, 1)

            def weigh_values(t, par, g):
                kind, g4 = (CROSS, SELF)[g // 4], g % 4
                pe.wait_ge(exp_done, t * NC2 + LAST_CHUNK[g] + 1)
                if kind == SELF:
                    pe.wait_ge(mask_done, t * SELF_C2 + 3 * g4 + 3)
                if g % 2 == 0:
                    ge(pe, pv_copied, t * 4 + g // 2)
                col = (g % 2) * T
                for kt in range(NQ):
                    for n in range(4):
                        chunk, at = [(c, h0) for c, (kd, k_, h0, nh, q0) in enumerate(S2_CHUNKS)
                                     if kd == kind and k_ == kt and h0 <= 4 * g4 + n < h0 + nh][0]
                        nh, q0 = S2_CHUNKS[chunk][3:]
                        p = probs[:, chunk % NP, :].rearrange("p (h q) -> p h q", h=nh)[:, 4 * g4 + n - at, :]
                        last = pe.matmul(pv_bank[32 * n:32 * n + VW, col + q0:col + T], v_ext[:, par, kind, kt, 4 * g4 + n, :], p,
                                         start=kt == 0, stop=kt == NQ - 1, tile_position=(0, 32 * n))
                last.then_inc(pv_done, 1)

            def own(t, name):
                ge(pe, misc_free, misc_number(t, name))

            def transposes(dst, src):
                for n in range(NQ):
                    last = pe.transpose(dst[:, n * 128:(n + 1) * 128], src(n), ident[:, :])
                return last

            def misc_use(t, par, name, off):
                b, p1 = t + off, 1 - par
                own(t, name)
                if name == "xnT":
                    pe.wait_ge(xn_done, b + 1)
                    last = transposes(misc, lambda n: xn[:, n, :])
                elif name == "qproj":
                    pe.wait_ge(misc_free, misc_number(t, "xnT") + 1)
                    pe.matmul(misc[:, 0:T], w_q, xnT[:, :], start=True, stop=True)
                    last = pe.matmul(misc[:, T:2 * T], w_cq, xnT[:, :], start=True, stop=True)
                elif name == "kproj":
                    pe.wait_ge(x_loaded, b * 32 + 32)
                    pe.matmul(misc[:, 0:T], w_k, xnT[:, :], start=True, stop=True)
                    last = pe.matmul(misc[:, T:2 * T], w_ck, ctx_in[:, p1, :], start=True, stop=True)
                elif name == "vproj":
                    for n in range(NQ):
                        pe.matmul(misc[:, n * 128:(n + 1) * 128], xnT[:, n * 128:(n + 1) * 128], w_v, start=True, stop=True)
                    for n in range(NQ):
                        last = pe.matmul(misc[:, T + n * 128:T + (n + 1) * 128], ctx_in[:, p1, n * 128:(n + 1) * 128], w_cv,
                                         start=True, stop=True)
                elif name in ("shift_cross", "shift_self"):
                    kind = CROSS if name == "shift_cross" else SELF
                    pe.wait_ge(max_taken, b * NC1 + (CROSS_C1 if kind == CROSS else NC1))
                    for n in range(NQ):
                        last = pe.transpose(misc[0:H, n * 128:(n + 1) * 128], row_max[:, kind, n, :], ident[:, :])
                elif name in ("y0", "y1", "y2", "y3"):
                    i = int(name[1])
                    pe.wait_ge(pv_copied, b * 4 + i + 1)
                    for qt in range(NQ):
                        for g in range(2):
                            last = pe.transpose(misc[:, (qt * 2 + g) * 128:(qt * 2 + g + 1) * 128],
                                                y_raw[:, i % 2, g * T + qt * 128:g * T + (qt + 1) * 128], ident[:, :])
                elif name == "yT":
                    pe.wait_ge(y_done, b + 1)
                    last = transposes(misc, lambda n: y[:, n, :])
                elif name == "wp":
                    pe.wait_ge(misc_free, misc_number(t, "yT") + 1)
                    for n in range(NQ):
                        last = pe.matmul(misc[:, n * 128:(n + 1) * 128], yT[:, n * 128:(n + 1) * 128], w_p, start=True, stop=True)
                elif name == "xn2T":
                    pe.wait_ge(xn2_done, b + 1)
                    last = transposes(misc, lambda n: xn2[:, n, :])
                elif name == "logits":
                    pe.wait_ge(misc_free, misc_number(t, "xn2T") + 1)
                    for n in range(NQ):
                        last = pe.matmul(misc[:, n * E:(n + 1) * E], xn2T[:, n * 128:(n + 1) * 128], w_router, start=True, stop=True)
                elif name == "combT":
                    pe.wait_ge(comb_done, b + 1)
                    for n in range(NQ):
                        last = pe.transpose(misc[0:E, n * 128:(n + 1) * 128], r_w[:, n, :], ident[:, :])
                last.then_inc(misc_ready, 1)

            def gate_up(b, j):
                if j:
                    pe.wait_ge(f_h_done, b * NB + j)
                e0 = slice(j * 128, (j + 1) * 128)
                pe.matmul(gu_bank[:, 0:T], w_gate[:, e0], xn2T[:, :], start=True, stop=True)
                pe.matmul(gu_bank[:, T:2 * T], w_up[:, e0], xn2T[:, :], start=True, stop=True).then_inc(gu_ready, 1)

            def down(b, j):
                pe.wait_ge(f_hc_done, b * NB + j + 1)
                for n in range(NQ):
                    last = pe.matmul(down_bank[:, n * 128:(n + 1) * 128], f_hc[:, j, n * 128:(n + 1) * 128], w_down[:, j, :],
                                     start=j == 0 and n == 0, stop=j == NB - 1 and n == NQ - 1)
                last.then_inc(down_used, 1)

            def tick(t, par):
                for what, n in steps("pe"):
                    if what == "max":
                        off = 0 if n >= CROSS_C1 else 1
                        if on(t + off):
                            max_chunk(t + off, (par + off) % 2, n)
                    elif what == "exp" and on(t):
                        exp_chunk(t, par, n)
                    elif what == "pv" and on(t):
                        weigh_values(t, par, n)
                    elif what == "gate_up" and on(t - 1):
                        gate_up(t - 1, n)
                    elif what == "down" and on(t - 1):
                        down(t - 1, n)
                    elif what in MISC_BATCH and on(t + MISC_BATCH[what]):
                        misc_use(t, par, what, MISC_BATCH[what])
                if isinstance(t, int) and t == FIRST_TICK:
                    pe.wait_ge(w_experts, 32)

            ticks(pe, tick)

        @block.vector
        def _(dve):
            for pads in (r_gin, r_gtop, r_ein, r_etop):
                nc.vector.memset(pads[:, :, :], PAD)

            def scale_constants():
                dve.wait_ge(w_first, 48)
                nc.vector.tensor_scalar(bias_q[:, :], cols_sb[:, 0:2], SCALE, None, ALU.mult)
                nc.vector.tensor_tensor(bias_v[:, :], cols_sb[:, 4:5], cols_sb[:, 5:6], ALU.add).then_inc(scaled, 1)
                dve.wait_ge(gate_made, 1)
                nc.vector.tensor_scalar(gate[:, 2:3], gate[:, 1:2], ROUTED_SCALE / 2, None, ALU.mult).then_inc(gate_made, 1)
                nc.vector.tensor_scalar(bp_row[:, :], rows_sb[:, 0:C], gate[:, 0:1], None, ALU.mult).then_inc(gate_made, 1)

            def clear_stack(st, n, kind):
                words = st[64:128, n, kind].rearrange("p h t -> p (h t)").bitcast(mybir.dt.uint32)
                nc.vector.memset(words, 0).then_inc(stack_cleared, 1)

            def stats(src, st, mv, step, done):
                for n in range(NQ):
                    nc.vector.bn_stats(st[:, n, :], src[:, n, :]).then_inc(step, 1)
                dve.wait_ge(step, NQ)
                dve.sem_clear(step)
                for n in range(NQ):
                    last = nc.vector.bn_aggr(mv[:, n, :], st[:, n, :])
                last.then_inc(done, 1)

            def normalise(src, mv, rs, dst, done):
                for n in range(NQ):
                    last = nc.vector.tensor_scalar(dst[:, n, :], src[:, n, :], mv[:, n, 0:1], rs[:, n:n + 1], ALU.subtract, ALU.mult)
                last.then_inc(done, 1)

            def take_max(b, k):
                kind, qt, h0, nh, keys = S1_CHUNKS[k]
                dve.wait_ge(max_scores, b * NC1 + k + 1)
                nc.vector.tensor_reduce(row_max[:, kind, qt, h0:h0 + nh], max_bank[k % 2][:, :].rearrange("p (h k) -> p h k", h=nh),
                                        AX.X, ALU.max).then_inc(max_taken, 1)

            def shift(t, b, name, kind):
                dve.wait_ge(misc_ready, misc_number(t, name) + 1)
                ge(dve, shift_in[kind], b * 16)
                nc.vector.tensor_scalar(shiftT[:, kind, :], misc[0:H, 0:T], -1.0, None, ALU.mult).then_inc(misc_free, 1)

            def merge(t, b, i):
                dve.wait_ge(misc_ready, misc_number(t, f"y{i}") + 1)
                v = misc[:, :].rearrange("p (a v) -> p a v", v=VW)
                nc.vector.reciprocal(recip[:, :].unsqueeze(2), v[:, :, SUM_COL:SUM_COL + 1]).then_inc(y_step, 1)
                dve.wait_ge(y_step, 1)
                dve.sem_clear(y_step)
                half = slice((i % 2) * C // 2, (i % 2 + 1) * C // 2)
                r = recip[:, :].unsqueeze(2).broadcast_to([128, 16, D])
                if i < 2:
                    if i == 0:
                        ge(dve, misc_ready, misc_batch_number(b - 1, "yT") + 1 if not isinstance(b, int) or b > 0 else 0)
                    o = y[:, :, half].rearrange("p n (a d) -> p n a d", d=D)
                    nc.vector.tensor_tensor(o, v[:, :, 0:D].rearrange("p (n a) d -> p n a d", n=NQ),
                                            r.rearrange("p (n a) d -> p n a d", n=NQ), ALU.mult).then_inc(misc_free, 1)
                else:
                    nc.vector.tensor_tensor(y_tmp[:, :, :].rearrange("p n (a d) -> p (n a) d", d=D), v[:, :, 0:D], r,
                                            ALU.mult).then_inc(misc_free, 1)
                    dve.wait_ge(misc_free, misc_number(t, f"y{i}") + 1)
                    last = nc.vector.tensor_tensor(y[:, :, half], y[:, :, half], y_tmp[:, :, :], ALU.add)
                    if i == 3:
                        last.then_inc(y_done, 1)

            def first_stats(b, p):
                dve.wait_ge(x_loaded, b * 32 + 32)
                stats(x_in[:, p], stats1, mean1, ln1_step, stats_done)

            def first_norm(b, p):
                dve.wait_ge(rstd_done, b + 1)
                if not isinstance(b, int) or b:
                    dve.wait_ge(misc_ready, misc_batch_number(b - 1, "xnT") + 1)
                normalise(x_in[:, p], mean1, rstd1, xn, xn_done)

            def split_queries(t, b, n):
                src, rem, prt = proj[:, 0, :], rest[:, 0, :], part[:, 0]
                if n == 0:
                    dve.wait_ge(misc_free, misc_number(t, "qproj") + 1)
                    ge(dve, q_stored, b * 48)
                    nc.vector.tensor_copy(prt[:, 0, :], src).then_inc(q_split, 1)
                elif n == 1:
                    dve.wait_ge(q_split, b * PARTS + 1)
                    nc.vector.tensor_tensor(rem, src, prt[:, 0, :], ALU.subtract).then_inc(q_rest, 1)
                elif n == 2:
                    dve.wait_ge(q_rest, 1)
                    dve.sem_clear(q_rest)
                    nc.vector.tensor_copy(prt[:, 1, :], rem).then_inc(q_split, 1)
                else:
                    dve.wait_ge(q_split, b * PARTS + 2)
                    nc.vector.tensor_tensor(prt[:, 2, :], rem, prt[:, 1, :], ALU.subtract).then_inc(q_split, 1)

            def route(t, b, n):
                grouped = r_choice[:, :, :].rearrange("p n (g e) -> p (n g) e", g=GROUPS)
                by_group = lambda a: a.rearrange("p n (g e) -> p n g e", g=GROUPS)
                per_expert = lambda a: a.unsqueeze(3).broadcast_to([128, NQ, GROUPS, E // GROUPS])
                if n == 0:
                    dve.wait_ge(misc_free, misc_number(t, "logits") + 1)
                else:
                    dve.wait_ge(route_step, n)
                if n == 0:
                    last = nc.vector.tensor_scalar(r_score[:, :, :], r_tanh[:, :, :], 0.5, 0.5, ALU.mult, ALU.add)
                elif n == 1:
                    last = nc.vector.tensor_tensor(r_choice[:, :, :], r_score[:, :, :], rb_row[:, :].unsqueeze(1).broadcast_to([128, NQ, E]),
                                                   ALU.add)
                elif n == 2:
                    nc.vector.tensor_tensor(r_pair[:, :, 0:3], grouped[:, :, 0:3], grouped[:, :, 1:4], ALU.add)
                    nc.vector.tensor_tensor(r_pair[:, :, 3:5], grouped[:, :, 0:2], grouped[:, :, 2:4], ALU.add)
                    last = nc.vector.tensor_tensor(r_pair[:, :, 5:6], grouped[:, :, 0:1], grouped[:, :, 3:4], ALU.add)
                elif n == 3:
                    last = nc.vector.tensor_reduce(r_gin[:, :, 0:GROUPS], r_pair[:, :, :].rearrange("p (n g) k -> p n g k", n=NQ), AX.X, ALU.max)
                elif n == 4:
                    for m in range(NQ):
                        last = nc.vector.max(r_g8[:, m, :], r_gin[:, m, :])
                elif n == 5:
                    last = nc.vector.tensor_copy(r_gtop[:, :, 0:TOP_GROUPS], r_g8[:, :, 0:TOP_GROUPS])
                elif n == 6:
                    for m in range(NQ):
                        last = nc.vector.match_replace(r_gout[:, m, :], r_gtop[:, m, :], r_gin[:, m, :], TAKEN)
                elif n == 7:
                    last = nc.vector.tensor_scalar(r_gsel[:, :, :], r_gout[:, :, 0:GROUPS], TAKEN, None, ALU.is_equal)
                elif n == 8:
                    nc.vector.tensor_scalar(r_gpen[:, :, :], r_gsel[:, :, :], -NEG_INF, NEG_INF, ALU.mult, ALU.add)
                    last = nc.vector.tensor_tensor(by_group(r_ein[:, :, 0:E]), by_group(r_choice[:, :, :]), per_expert(r_gsel[:, :, :]), ALU.mult)
                elif n == 9:
                    o = by_group(r_ein[:, :, 0:E])
                    last = nc.vector.tensor_tensor(o, o, per_expert(r_gpen[:, :, :]), ALU.add)
                elif n == 10:
                    for m in range(NQ):
                        last = nc.vector.max(r_e8[:, m, :], r_ein[:, m, :])
                elif n == 11:
                    last = nc.vector.tensor_copy(r_etop[:, :, 0:TOP_EXPERTS], r_e8[:, :, 0:TOP_EXPERTS])
                elif n == 12:
                    for m in range(NQ):
                        last = nc.vector.match_replace(r_eout[:, m, :], r_etop[:, m, :], r_ein[:, m, :], TAKEN)
                elif n == 13:
                    ge(dve, misc_ready, misc_batch_number(b - 1, "combT") + 1 if not isinstance(b, int) or b > 0 else 0)
                    last = nc.vector.scalar_tensor_tensor(out=r_sel[:, :, :], in0=r_eout[:, :, 0:E], scalar=TAKEN, in1=r_score[:, :, :],
                                                          op0=ALU.is_equal, op1=ALU.mult)
                elif n == 14:
                    last = nc.vector.tensor_reduce(r_sum[:, :], r_sel[:, :, :], AX.X, ALU.add)
                elif n == 15:
                    last = nc.vector.tensor_scalar(r_sum[:, :], r_sum[:, :], 1e-20, None, ALU.add)
                elif n == 16:
                    last = nc.vector.reciprocal(r_sum[:, :], r_sum[:, :])
                else:
                    dve.sem_clear(route_step)
                    nc.vector.scalar_tensor_tensor(out=r_w[:, :, :], in0=r_sel[:, :, :], scalar=gate[:, 2:3],
                                                   in1=r_sum[:, :].unsqueeze(2).broadcast_to([128, NQ, E]),
                                                   op0=ALU.mult, op1=ALU.mult).then_inc(comb_done, 1)
                if n < ROUTE_STEPS - 1:
                    last.then_inc(route_step, 1)

            def swish(b, j):
                dve.wait_ge(f_tanh_done, b * NB + j + 1)
                nc.vector.scalar_tensor_tensor(out=f_gate[:, :], in0=f_tanh[:, :], scalar=1.0, in1=gu_bank[:, 0:T],
                                               op0=ALU.add, op1=ALU.mult).then_inc(f_gate_done, 1)

            def times_up(b, j):
                dve.wait_ge(f_gate_done, b * NB + j + 1)
                nc.vector.tensor_tensor(f_h[:, j, :], f_gate[:, :], gu_bank[:, T:2 * T], ALU.mult).then_inc(f_h_done, 1)

            def tick(t, par):
                for what, n in steps("dve"):
                    if what == "y" and on(t if n < 3 else t - 1):
                        merge(t, t if n < 3 else t - 1, n)
                    elif what == "max":
                        off = 0 if n >= CROSS_C1 else 1
                        if on(t + off):
                            take_max(t + off, n)
                    elif what == "x1" and on(t - 1):
                        dve.wait_ge(misc_ready, misc_number(t, "wp") + 1)
                        dve.wait_ge(res_done, t)
                        nc.vector.scalar_tensor_tensor(out=x1[:, :, :], in0=misc[:, 0:T].rearrange("p (n c) -> p n c", n=NQ),
                                                       scalar=gate[:, 0:1], in1=x_res[:, 1 - par], op0=ALU.mult, op1=ALU.add)\
                            .then_inc(misc_free, 1)
                    elif what == "stats2" and on(t - 1):
                        dve.wait_ge(misc_free, misc_number(t, "wp") + 1)
                        stats(x1, stats2, mean2, ln2_step, stats2_done)
                    elif what == "queries" and on(t + 1):
                        split_queries(t, t + 1, n)
                        if isinstance(t, int) and t == FIRST_TICK and n == PARTS:
                            for st in (q_stack, k_stack):
                                for kind in (SELF, CROSS):
                                    clear_stack(st, 1, kind)
                    elif what == "xn2" and on(t - 1):
                        b = t - 1
                        dve.wait_ge(rstd2_done, b + 1)
                        ge(dve, misc_ready, misc_batch_number(b - 1, "xn2T") + 1 if not isinstance(b, int) or b > 0 else 0)
                        normalise(x1, mean2, rstd2, xn2, xn2_done)
                    elif what == "route" and on(t - 1):
                        route(t, t - 1, n)
                    elif what == "shift_self" and on(t):
                        shift(t, t, "shift_self", SELF)
                    elif what == "shift_cross" and on(t + 1):
                        shift(t, t + 1, "shift_cross", CROSS)
                    elif what == "swish" and on(t - 1):
                        swish(t - 1, n)
                    elif what == "times_up" and on(t - 1):
                        times_up(t - 1, n)
                    elif what == "stats1" and on(t + 2):
                        first_stats(t + 2, par)
                    elif what == "xn1" and on(t + 2):
                        first_norm(t + 2, par)
                    elif what == "out" and on(t - 1):
                        b = t - 1
                        dve.wait_ge(down_used, b * NB + NB)
                        dve.wait_ge(stored, b * 16 + 16)
                        nc.vector.tensor_tensor(y_out[:, :, :], down_bank[:, 0:T].rearrange("p (n c) -> p n c", n=NQ), x1[:, :, :],
                                                ALU.add).then_inc(out_done, 1)

            clear_stack(q_stack, 0, CROSS)
            first_stats(0, 0)
            first_norm(0, 0)
            scale_constants()
            clear_stack(q_stack, 0, SELF)
            ticks(dve, tick)


_P = "L0_xattn_"
_F = "L0_ffn_"


def kernel(**inputs):
    import numpy as np
    import concourse.bacc as bacc
    from concourse.bass_utils import run_bass_kernel_spmd

    a = {k: np.asarray(v) for k, v in inputs.items()}
    p = lambda n: a[_P + n]
    by_d = lambda w: w.reshape(w.shape[:-1] + (H, D)).swapaxes(-1, -2).reshape(w.shape)
    ins = {
        "x": a["x"], "ctxT": a["ctx_512"].transpose(2, 0, 1),
        "w_model": np.concatenate([by_d(p("Wq")), by_d(p("Wcq")), by_d(p("Wk")), p("Wv"), p("Wp"), a[_F + "router_weight"].T], axis=1),
        "w_ctx": np.concatenate([by_d(p("Wck")), p("Wcv")], axis=1),
        "cols": np.stack([by_d(p(n)) for n in ("bq", "bcq", "bk", "bck")] + [p("bv"), p("bcv")], axis=1),
        "rows": np.concatenate([p("bp"), a[_F + "router_bias"], a["g_xattn"], a["g_ffn"]]),
        "w_pairs": np.stack([a[_F + n].transpose(2, 0, 1).reshape(C, E * I) for n in ("w_gate", "w_up")], axis=1),
        "w_down": a[_F + "w_down"].transpose(0, 2, 1).reshape(NB, 128, C).transpose(1, 0, 2),
    }
    nc = bacc.Bacc("TRN2", target_bir_lowering=False, num_devices=1)
    arrays, args = {}, []
    for name, v in ins.items():
        v = np.ascontiguousarray(v)
        arrays["in_" + name] = v
        args.append(nc.dram_tensor("in_" + name, v.shape, mybir.dt.from_np(v.dtype), kind="ExternalInput").ap())
    out = nc.dram_tensor("out", (B, T, C), FP32, kind="ExternalOutput").ap()
    build(nc, *args, out)
    r = run_bass_kernel_spmd(nc, [arrays], core_ids=[0])
    return r.results[0]["out"]
```

```python
import concourse.bass as bass
from concourse import mybir
from contextlib import ExitStack

FP32 = mybir.dt.float32
BF16 = mybir.dt.bfloat16
ALU = mybir.AluOpType
ACT = mybir.ActivationFunctionType
AX = mybir.AxisListType

B, T, C, CC, H, E, I = 8, 256, 128, 64, 16, 16, 64
D = C // H
NQ = T // 128
SCALE = D ** -0.5
EPS = 1e-5
NEG_INF = -1e9
MASKED = -1e30
PAD = -3e38
TAKEN = -2e38
TOP_GROUPS, TOP_EXPERTS, GROUPS = 2, 4, 4
ROUTED_SCALE = 2.5

PARTS = 3
STACK = PARTS * PARTS * D
SHIFT_ROW = STACK
VW = 32
SUM_COL = D

SELF, CROSS = 0, 1
NB = E * I // 128

S2_CHUNKS = []
S2_GROUP = []
for g in range(H // 4):
    S2_CHUNKS += [(CROSS, kt, 4 * g + hp, 2, 0) for kt in range(NQ) for hp in (0, 2)]
    S2_GROUP += [g] * 4
for g in range(H // 4):
    S2_CHUNKS += [(SELF, 0, 4 * g, 2, 0), (SELF, 0, 4 * g + 2, 2, 0), (SELF, 1, 4 * g, 4, 128)]
    S2_GROUP += [H // 4 + g] * 3
NC2 = len(S2_CHUNKS)
CROSS_C2 = 4 * (H // 4)
SELF_C2 = NC2 - CROSS_C2
LAST_CHUNK = [max(c for c in range(NC2) if S2_GROUP[c] == g) for g in range(8)]
NP = 7
assert NC2 % NP == 0 and NC2 % 2 == 0

S1_CHUNKS = [(CROSS, qt, 2 * g, 2, 256) for qt in range(NQ) for g in range(8)]
CROSS_C1 = len(S1_CHUNKS)
S1_CHUNKS += [(SELF, 0, 4 * g, 4, 128) for g in range(4)] + [(SELF, 1, 2 * g, 2, 256) for g in range(8)]
NC1 = len(S1_CHUNKS)

FIRST_TICK, LOOP_LO, LOOP_HI, LAST_TICK = -1, 1, 7, B

ORDERS = {
    'pe': '''
        max:16 y3 xnT max:17 qproj exp:0 max:18 max:19 kproj max:20 yT exp:1 max:21 exp:2 wp exp:3 max:22 max:23 exp:4 vproj
        exp:5 pv:0 max:24 exp:6 max:25 exp:7 xn2T max:26 exp:8 exp:9 pv:1 max:27 exp:10 logits exp:11 gate_up:0 shift_self
        exp:12 gate_up:1 exp:13 y0 max:0 max:1 exp:14 pv:2 max:2 exp:15 max:3 exp:16 gate_up:2 max:4 exp:17 max:5 max:6 pv:3
        max:7 combT exp:18 max:8 exp:19 max:9 gate_up:3 gate_up:4 exp:20 max:10 pv:4 exp:21 max:11 exp:22 max:12 gate_up:5
        exp:23 y1 exp:24 max:13 exp:25 pv:5 exp:26 max:14 gate_up:6 max:15 exp:27 y2 pv:6 gate_up:7 shift_cross pv:7 down''',
    'act': '''
        xnT qproj q_part0 exp:0 kproj k_part0 yT exp:1 exp:2 exp:3 exp:4 exp:5 vproj exp:6 exp:7 xn2T exp:8 exp:9 exp:10 logits
        exp:11 tanh:0 shift_self pv_copy:0 exp:12 exp:13 exp:14 exp:15 tanh:1 exp:16 exp:17 combT tanh:2 exp:18 pv_copy:1 exp:19
        tanh:3 exp:20 exp:21 exp:22 tanh:4 exp:23 exp:24 exp:25 tanh:5 pv_copy:2 tanh:6 exp:26 exp:27 shift_cross tanh:7
        pv_copy:3''',
    'dve': '''
        max:16 y:3 max:17 max:18 max:19 queries:1 max:20 queries:2 queries:3 max:21 x1 stats2 max:22 max:23 xn2 max:24 max:25
        max:26 max:27 route:0 route:1 route:2 route:3 swish:0 route:4 route:5 times_up:0 route:6 route:7 y:0 route:8 max:0
        route:9 max:1 route:10 route:11 route:12 route:13 max:2 route:14 max:3 route:15 max:4 max:5 route:16 swish:1 route:17
        max:6 max:7 times_up:1 swish:2 times_up:2 max:8 swish:3 max:9 times_up:3 max:10 max:11 max:12 swish:4 y:1 times_up:4
        max:13 stats1 swish:5 max:14 max:15 times_up:5 y:2 swish:6 times_up:6 swish:7 times_up:7 out''',
    'pool': '''
        keys:1 keys:2 rstd2 keys:3 mask:16 mask:17 mask:18 mask:19 mask:20 mask:21 mask:22 mask:23 mask:24 weight:0 weight:1
        mask:25 mask:26 weight:2 mask:27 weight:3 weight:4 weight:5 weight:6 weight:7 rstd1 xn1 residual''',
    'sp': '''
        shift_rows q_part:0 q_part:1 q_part:2 load k_part:0 k_part:1 k_part:2 q_stack:1 k_stack:1 shift_self k_stack:0 comb_out
        comb_in q_stack:0 shift_cross out''',
    'pe_first': '''
        xnT qproj kproj vproj max:0 max:1 max:2 max:3 max:4 max:5 max:6 max:7 max:8 max:9 max:10 max:11 max:12 max:13 max:14
        max:15 shift_cross''',
    'pe_last': '''
        y3 yT wp xn2T logits gate_up:0 gate_up:1 combT gate_up:2 gate_up:3 gate_up:4 gate_up:5 gate_up:6 gate_up:7 down''',
    'act_first': '''
        xnT qproj q_part0 kproj k_part0 vproj shift_cross''',
    'act_last': '''
        yT xn2T logits tanh:0 tanh:1 combT tanh:2 tanh:3 tanh:4 tanh:5 tanh:6 tanh:7''',
    'dve_first': '''
        queries:1 queries:2 queries:3 keys:1 keys:2 keys:3 max:0 max:1 max:2 max:3 stats1 max:4 max:5 max:6 max:7 max:8 max:9
        max:10 max:11 max:12 max:13 max:14 max:15''',
    'dve_last': '''
        y:3 x1 stats2 xn2 route:0 route:1 route:2 route:3 route:4 route:5 route:6 route:7 swish:0 route:8 route:9 times_up:0
        route:10 route:11 route:12 swish:1 route:13 route:14 route:15 route:16 route:17 times_up:1 swish:2 times_up:2 swish:3
        times_up:3 swish:4 times_up:4 swish:5 times_up:5 swish:6 times_up:6 swish:7 times_up:7 out''',
    'pool_first': '''
        rstd1 residual xn1''',
    'pool_last': '''
        rstd2 weight:0 weight:1 weight:2 weight:3 weight:4 weight:5 weight:6 weight:7''',
    'sp_first': '''
        shift_rows q_part:0 q_part:1 q_part:2 load k_part:0 q_stack:1 k_part:1 k_part:2 k_stack:1 q_stack:0 k_stack:0
        shift_cross''',
    'sp_last': '''
        comb_out comb_in out''',
}


def order(engine, t):
    words = ORDERS[engine + {FIRST_TICK: "_first", LAST_TICK: "_last"}.get(t, "")] if isinstance(t, int) else ORDERS[engine]
    return [(w.partition(":")[0], int(w.partition(":")[2] or 0)) for w in words.split()]


MISC_BATCH = dict(xnT=1, qproj=1, kproj=1, vproj=1, shift_cross=1, shift_self=0, y0=0, y1=0, y2=0, y3=-1, yT=-1, wp=-1,
                  xn2T=-1, logits=-1, combT=-1, down=-1)
ROUTE_STEPS = 18


def on(b):
    return not isinstance(b, int) or 0 <= b < B


def misc_number(t, name):
    uses = lambda u: [what for what, _ in order("pe", u) if what in MISC_BATCH and on(u + MISC_BATCH[what])]
    if isinstance(t, int):
        return sum(len(uses(u)) for u in range(FIRST_TICK, t)) + uses(t).index(name)
    steady = [what for what, _ in order("pe", LOOP_LO) if what in MISC_BATCH]
    before = sum(len(uses(u)) for u in range(FIRST_TICK, LOOP_LO))
    return (t - LOOP_LO) * len(steady) + (before + steady.index(name))


def misc_batch_number(b, name):
    off = MISC_BATCH[name]
    return misc_number(b - off, name)


def build(nc, x, ctxT, w_model, w_ctx, cols, rows, w_pairs, w_down_in, out):
    stack = ExitStack()
    with stack:
        def sb(name, shape, dt=FP32):
            return stack.enter_context(nc.sbuf_tensor(name, shape, dt))

        def sem(name):
            return stack.enter_context(nc.semaphore(name))

        w_model_sb = sb("w_model_sb", [C, 5 * C + E])
        w_q, w_cq, w_k, w_v, w_p = (w_model_sb[:, n * C:(n + 1) * C] for n in range(5))
        w_router = w_model_sb[:, 5 * C:5 * C + E]
        w_ctx_sb = sb("w_ctx_sb", [CC, 2 * C])
        w_ck, w_cv = w_ctx_sb[:, 0:C], w_ctx_sb[:, C:2 * C]
        w_pairs_sb = sb("w_pairs_sb", [C, 2, E * I])
        w_gate, w_up = w_pairs_sb[:, 0, :], w_pairs_sb[:, 1, :]
        w_down = sb("w_down", [128, NB, C])
        cols_sb = sb("cols_sb", [C, 6])
        bias_q = sb("bias_q", [C, 2])
        bias_v = sb("bias_v", [C, 1])
        rows_sb = sb("rows_sb", [128, C + E + 2])
        rb_row, gates = rows_sb[:, C:C + E], rows_sb[:, C + E:C + E + 2]
        bp_row = sb("bp_row", [128, C])
        gate = sb("gate", [128, 3])
        minus_half = sb("minus_half", [128, NQ])
        ident = sb("ident", [128, 128])
        ident_b = sb("ident_b", [128, 128], BF16)
        causal = sb("causal", [128, 4, 128], BF16)
        zero_row = sb("zero_row", [2 * H, T], BF16)
        ones_row = sb("ones_row", [2 * H, T], BF16)

        x_in = sb("x_in", [128, 2, NQ, C])
        ctx_in = sb("ctx_in", [CC, 2, T])
        stats1, mean1, rstd1 = sb("stats1", [128, NQ, 6]), sb("mean1", [128, NQ, 2]), sb("rstd1", [128, NQ])
        xn = sb("xn", [128, NQ, C])
        xnT = sb("xnT", [C, T])
        proj = sb("proj", [C, 2, 2 * T])
        rest = sb("rest", [C, 2, 2 * T])
        part = sb("part", [C, 2, PARTS, 2 * T], BF16)
        q_stack = sb("q_stack", [128, 2, 2, H, T], BF16)
        k_stack = sb("k_stack", [128, 2, 2, H, T], BF16)
        v_ext = sb("v_ext", [128, 2, 2, NQ, H, VW])
        row_max = sb("row_max", [128, 2, NQ, H])
        shiftT = sb("shiftT", [H, 2, T], BF16)
        probs = sb("probs", [128, NP, 512])
        y_raw = sb("y_raw", [128, 2, 512])
        recip = sb("recip", [128, 16])
        y_tmp = sb("y_tmp", [128, NQ, C // 2])
        y = sb("y", [128, NQ, C])
        yT = sb("yT", [C, T])
        x_res = sb("x_res", [128, 2, NQ, C])
        x1 = sb("x1", [128, NQ, C])
        stats2, mean2, rstd2 = sb("stats2", [128, NQ, 6]), sb("mean2", [128, NQ, 2]), sb("rstd2", [128, NQ])
        xn2 = sb("xn2", [128, NQ, C])
        xn2T = sb("xn2T", [C, T])
        r_tanh, r_score, r_choice = (sb(n, [128, NQ, E]) for n in ("r_tanh", "r_score", "r_choice"))
        r_pair = sb("r_pair", [128, NQ * GROUPS, 6])
        r_gin, r_gout = sb("r_gin", [128, NQ, 10]), sb("r_gout", [128, NQ, 10])
        r_g8, r_gtop = sb("r_g8", [128, NQ, 8]), sb("r_gtop", [128, NQ, 8])
        r_gsel, r_gpen = sb("r_gsel", [128, NQ, GROUPS]), sb("r_gpen", [128, NQ, GROUPS])
        r_ein, r_eout = sb("r_ein", [128, NQ, 20]), sb("r_eout", [128, NQ, 20])
        r_e8, r_etop = sb("r_e8", [128, NQ, 8]), sb("r_etop", [128, NQ, 8])
        r_sel, r_w = sb("r_sel", [128, NQ, E]), sb("r_w", [128, NQ, E])
        r_sum = sb("r_sum", [128, NQ])
        combT = sb("combT", [E, T])
        comb = sb("comb", [128, NB, T])
        f_tanh, f_gate = sb("f_tanh", [128, 2, T]), sb("f_gate", [128, 2, T])
        f_h, f_hc = sb("f_h", [128, NB, T]), sb("f_hc", [128, NB, T])
        y_out = sb("y_out", [128, NQ, C])

        q_scr = nc.dram_tensor("q_scr", (2, 2, PARTS, D, H, T), BF16).ap()
        k_scr = nc.dram_tensor("k_scr", (2, 2, PARTS, D, H, T), BF16).ap()
        c_scr = nc.dram_tensor("c_scr", (E, T), FP32).ap()

        bank = [stack.enter_context(nc.psum_tensor(f"bank{n}", [128, 512], FP32)) for n in range(8)]
        max_bank, exp_bank, pv_bank, gu_bank, misc = bank[0:2], bank[2:4], bank[4], bank[5:7], bank[7]

        w_first = sem("w_first")
        w_rows = sem("w_rows")
        w_experts = sem("w_experts")
        ones_in = sem("ones_in")
        v_cleared = sem("v_cleared")
        stack_cleared = sem("stack_cleared")
        const_made = sem("const_made")
        const_step = sem("const_step")
        scaled = sem("scaled")
        gate_made = sem("gate_made")
        x_loaded = sem("x_loaded")
        stats_done = sem("stats_done")
        rstd_done = sem("rstd_done")
        rstd_step = sem("rstd_step")
        xn_done = sem("xn_done")
        ln1_step, q_rest, split_step = sem("ln1_step"), sem("q_rest"), sem("split_step")
        q_split, k_split = sem("q_split"), sem("k_split")
        q_stored, k_stored = sem("q_stored"), sem("k_stored")
        shift_cleared = sem("shift_cleared")
        stack_in = [sem("stack_in_self"), sem("stack_in_cross")]
        res_done = sem("res_done")
        max_scores = sem("max_scores")
        max_taken = sem("max_taken")
        shift_in = [sem("shift_in_self"), sem("shift_in_cross")]
        exp_scores = sem("exp_scores")
        exp_done = sem("exp_done")
        mask_done = sem("mask_done")
        pv_done = sem("pv_done")
        pv_copied = sem("pv_copied")
        y_step = sem("y_step")
        y_done = sem("y_done")
        misc_ready = sem("misc_ready")
        misc_free = sem("misc_free")
        ln2_step = sem("ln2_step")
        stats2_done = sem("stats2_done")
        rstd2_done = sem("rstd2_done")
        rstd2_step = sem("rstd2_step")
        xn2_done = sem("xn2_done")
        route_step = sem("route_step")
        comb_done = sem("comb_done")
        comb_stored = sem("comb_stored")
        comb_in = sem("comb_in")
        gu_ready = sem("gu_ready")
        f_tanh_done = sem("f_tanh_done")
        f_gate_done = sem("f_gate_done")
        f_h_done = sem("f_h_done")
        f_hc_done = sem("f_hc_done")
        stored = sem("stored")
        pool_carrier, sp_carrier = sem("pool_carrier"), sem("sp_carrier")

        block = stack.enter_context(nc.Block())

        def ge(eng, s, v):
            if not isinstance(v, int) or v > 0:
                eng.wait_ge(s, v)

        def ticks(eng, tick):
            for t in range(FIRST_TICK, LOOP_LO):
                tick(t, t % 2)
            with eng.Fori(LOOP_LO, LOOP_HI, 2) as t:
                tick(t, LOOP_LO % 2)
                tick(t + 1, (LOOP_LO + 1) % 2)
            for t in range(LOOP_HI, LAST_TICK + 1):
                tick(t, t % 2)

        def split_keys(eng, b, n):
            src, rem, prt = proj[:, 1, :], rest[:, 1, :], part[:, 1]
            if n == 1:
                eng.wait_ge(k_split, b * PARTS + 1)
                eng.tensor_tensor(rem, src, prt[:, 0, :], ALU.subtract).then_inc(split_step, 1)
            elif n == 2:
                eng.wait_ge(split_step, 1)
                eng.sem_clear(split_step)
                eng.tensor_scalar(prt[:, 1, :], rem, 1.0, None, ALU.mult).then_inc(k_split, 1)
            else:
                eng.wait_ge(k_split, b * PARTS + 2)
                eng.tensor_tensor(prt[:, 2, :], rem, prt[:, 1, :], ALU.subtract).then_inc(k_split, 1)

        @block.sync
        def _(sp):
            def load_x(b, par):
                sp.dma_start(x_in[:, par], x[b].rearrange("(n p) c -> p n c", p=128)).then_inc(x_loaded, 16)
                sp.dma_start(ctx_in[:, par], ctxT[:, b]).then_inc(x_loaded, 16)

            load_x(0, 0)
            sp.dma_start(w_model_sb[:, :], w_model).then_inc(w_first, 16)
            sp.dma_start(w_ctx_sb[:, :], w_ctx).then_inc(w_first, 16)
            sp.dma_start(cols_sb[:, :], cols).then_inc(w_first, 16)
            sp.dma_start(rows_sb[:, :], rows.partition_broadcast(128)).then_inc(w_rows, 16)
            sp.dma_start(w_pairs_sb[:, :, :], w_pairs).then_inc(w_experts, 16)
            sp.dma_start(w_down[:, :, :], w_down_in).then_inc(w_experts, 16)

            def tick(t, par):
                b, p1 = t + 1, 1 - par
                for what, n in order("sp", t):
                    if what == "load" and on(t + 2):
                        ge(sp, x_loaded, (t + 2) * 32)
                        sp.sem_inc(sp_carrier, 1)
                        ge(sp, res_done, t + 1)
                        sp.sem_inc(sp_carrier, 1)
                        if on(t):
                            ge(sp, misc_free, misc_number(t - 1, "vproj") + 1)
                        load_x(t + 2 if isinstance(t, int) else (t + 2) % B, par)
                    elif what == "q_part" and on(b):
                        ge(sp, q_split, b * PARTS + n + 1)
                        sp.dma_start(q_scr[p1, :, n].rearrange("k d h x -> (d h) k x"), part[:, 0, n, :].rearrange("c (k x) -> c k x", k=2)).then_inc(q_stored, 16)
                    elif what == "k_part" and on(b):
                        ge(sp, k_split, b * PARTS + n + 1)
                        sp.dma_start(k_scr[p1, :, n].rearrange("k d h x -> (d h) k x"), part[:, 1, n, :].rearrange("c (k x) -> c k x", k=2)).then_inc(k_stored, 16)
                    elif what == "shift_rows" and on(b):
                        ge(sp, pv_done, (b - 1) * 8)
                        sp.sem_inc(sp_carrier, 1)
                        if isinstance(t, int) and b < 2:
                            sp.wait_ge(const_step, 6)
                            sp.wait_ge(stack_cleared, (3, 7)[b])
                            sp.dma_start(k_stack[SHIFT_ROW:SHIFT_ROW + 1, p1], ones_row[:, :]).then_inc(ones_in, 16)
                        sp.dma_start(q_stack[SHIFT_ROW:SHIFT_ROW + 1, p1], zero_row[:, :]).then_inc(shift_cleared, 16)
                    elif what == "q_stack" and on(b):
                        ge(sp, q_stored, b * 48 + 48)
                        for i in range(PARTS):
                            src = q_scr[p1, n, i].rearrange("d h x -> d (h x)").unsqueeze(0).broadcast_to([PARTS, D, H * T])
                            sp.dma_start(q_stack[i * PARTS * D:(i + 1) * PARTS * D, p1, n], src).then_inc(stack_in[n], 16)
                    elif what == "k_stack" and on(b):
                        ge(sp, k_stored, b * 48 + 48)
                        src = k_scr[p1, n].rearrange("j d h x -> (j d) (h x)").unsqueeze(0).broadcast_to([PARTS, PARTS * D, H * T])
                        sp.dma_start(k_stack[0:STACK, p1, n], src).then_inc(stack_in[n], 16)
                    elif what == "shift_self" and on(t):
                        ge(sp, misc_free, misc_number(t, "shift_self") + 1)
                        sp.dma_start(q_stack[SHIFT_ROW:SHIFT_ROW + 1, par, SELF], shiftT[:, SELF, :]).then_inc(shift_in[SELF], 16)
                    elif what == "shift_cross" and on(b):
                        ge(sp, misc_free, misc_number(t, "shift_cross") + 1)
                        sp.dma_start(q_stack[SHIFT_ROW:SHIFT_ROW + 1, p1, CROSS], shiftT[:, CROSS, :]).then_inc(shift_in[CROSS], 16)
                    elif what == "comb_out" and on(t - 1):
                        ge(sp, misc_free, misc_number(t, "combT") + 1)
                        sp.dma_start(c_scr, combT[:, :]).then_inc(comb_stored, 16)
                    elif what == "comb_in" and on(t - 1):
                        sp.wait_ge(comb_stored, t * 16)
                        for e2 in range(2):
                            src = c_scr.rearrange("(j e) t -> e j t", e=2)[e2].partition_broadcast(I)
                            sp.dma_start(comb[e2 * I:(e2 + 1) * I, :, :], src).then_inc(comb_in, 16)
                    elif what == "out" and on(t - 1):
                        ge(sp, misc_free, misc_number(t, "down") + 1)
                        sp.dma_start(out[t - 1].rearrange("(n p) c -> p n c", p=128), y_out[:, :, :]).then_inc(stored, 16)

            sp.sem_inc(stored, 16)
            ticks(sp, tick)
            sp.wait_ge(x_loaded, 32 * (LOOP_HI - 1 + 3))
            sp.wait_ge(stored, 16 * B + 16)
            sp.wait_ge(q_stored, 48 * B)
            sp.wait_ge(k_stored, 48 * B)
            sp.wait_ge(comb_stored, 16 * B)

        @block.gpsimd
        def _(pool):
            nc.gpsimd.memset(ident[:, :], 0.0).then_inc(const_step, 1)
            nc.gpsimd.memset(minus_half[:, :], -0.5).then_inc(const_step, 1)
            nc.gpsimd.memset(causal[:, :, :], 0.0).then_inc(const_step, 1)
            nc.gpsimd.memset(ident_b[:, :], 0.0).then_inc(const_step, 1)
            nc.gpsimd.memset(zero_row[:, :], 0.0).then_inc(const_step, 1)
            nc.gpsimd.memset(ones_row[:, :], 1.0).then_inc(const_step, 1)
            pool.wait_ge(const_step, 6)
            nc.gpsimd.affine_select(out=ident[:, :], in_=ident[:, :], compare_op=ALU.not_equal, fill=1.0, base=0,
                                    pattern=[[-1, 128]], channel_multiplier=1).then_inc(const_made, 1)
            nc.gpsimd.affine_select(out=ident_b[:, :], in_=ident_b[:, :], compare_op=ALU.not_equal, fill=1.0, base=0,
                                    pattern=[[-1, 128]], channel_multiplier=1).then_inc(const_made, 1)
            nc.gpsimd.affine_select(out=causal[:, :, :], in_=causal[:, :, :], compare_op=ALU.is_ge, fill=MASKED, base=0,
                                    pattern=[[0, 4], [-1, 128]], channel_multiplier=1).then_inc(const_made, 1)

            def clear_values():
                v = v_ext[:, :, :, :, :, :].rearrange("p a k n h v -> p (a k n h) v")
                nc.gpsimd.memset(v, 0.0).then_inc(const_step, 1)
                pool.wait_ge(const_step, 7)
                nc.gpsimd.memset(v[:, :, SUM_COL:SUM_COL + 1], 1.0).then_inc(v_cleared, 1)

            def rstd(mv, rs, ready, b, step, done):
                pool.wait_ge(ready, b + 1)
                pool.sem_inc(pool_carrier, 1)
                nc.gpsimd.tensor_scalar(rs[:, :], mv[:, :, 1], EPS, None, ALU.add).then_inc(step, 1)
                pool.wait_ge(step, 1)
                pool.sem_clear(step)
                nc.gpsimd.tensor_tensor(rs[:, :], rs[:, :], minus_half[:, :], ALU.pow).then_inc(done, 1)

            def first_norm(b, p):
                pool.wait_ge(rstd_done, b + 1)
                pool.sem_inc(pool_carrier, 1)
                if not isinstance(b, int) or b:
                    pool.wait_ge(misc_ready, misc_batch_number(b - 1, "xnT") + 1)
                    pool.sem_inc(pool_carrier, 1)
                for n in range(NQ):
                    last = nc.gpsimd.tensor_scalar(xn[:, n, :], x_in[:, p, n, :], mean1[:, n, 0:1], rstd1[:, n:n + 1], ALU.subtract, ALU.mult)
                last.then_inc(xn_done, 1)

            def mask(b, s):
                _, kt, h0, nh, q0 = S2_CHUNKS[s]
                pool.wait_ge(exp_done, b * NC2 + s + 1)
                pool.sem_inc(pool_carrier, 1)
                p = probs[:, s % NP, :].rearrange("p (h q) -> p h q", h=nh)[:, :, 0:128]
                nc.gpsimd.affine_select(out=p, in_=p, compare_op=ALU.is_ge, fill=0.0, base=0,
                                        pattern=[[0, nh], [1, 128]], channel_multiplier=-1).then_inc(mask_done, 1)

            def combine(b, j):
                pool.wait_ge(f_h_done, b * NB + j + 1)
                if j == 0:
                    pool.wait_ge(comb_in, b * 32 + 32)
                nc.gpsimd.tensor_tensor(f_hc[:, j, :], f_h[:, j, :], comb[:, j, :], ALU.mult).then_inc(f_hc_done, 1)

            def tick(t, par):
                for what, n in order("pool", t):
                    if what == "mask" and on(t):
                        mask(t, n)
                    elif what == "keys" and on(t + 1):
                        split_keys(nc.gpsimd, t + 1, n)
                    elif what == "rstd2" and on(t - 1):
                        rstd(mean2, rstd2, stats2_done, t - 1, rstd2_step, rstd2_done)
                    elif what == "rstd1" and on(t + 2):
                        rstd(mean1, rstd1, stats_done, t + 2, rstd_step, rstd_done)
                    elif what == "xn1" and on(t + 2):
                        first_norm(t + 2, par)
                    elif what == "residual" and on(t + 1):
                        b, p1 = t + 1, 1 - par
                        pool.wait_ge(x_loaded, b * 32 + 32)
                        if isinstance(t, int) and t == FIRST_TICK:
                            pool.wait_ge(gate_made, 3)
                        if on(b - 2):
                            ge(pool, misc_free, misc_number(t, "wp") + 1)
                        nc.gpsimd.tensor_tensor(x_res[:, p1], x_in[:, p1],
                                                bp_row[:, :].unsqueeze(1).broadcast_to([128, NQ, C]), ALU.add).then_inc(res_done, 1)
                    elif what == "weight" and on(t - 1):
                        combine(t - 1, n)

            rstd(mean1, rstd1, stats_done, 0, rstd_step, rstd_done)
            first_norm(0, 0)
            clear_values()
            ticks(pool, tick)

        @block.scalar
        def _(act):
            act.wait_ge(const_step, 2)
            words = k_stack[64:128, 0].rearrange("p k h t -> p (k h t)").bitcast(mybir.dt.float32)
            nc.scalar.activation(words, minus_half[64:128, 0:1].broadcast_to([64, words.shape[1]]), ACT.Copy, scale=0.0).then_inc(stack_cleared, 1)
            act.wait_ge(w_rows, 16)
            nc.scalar.activation(gate[:, 0:2], gates, ACT.Tanh).then_inc(gate_made, 1)
            def take(t, name):
                act.wait_ge(misc_ready, misc_number(t, name) + 1)

            def shift(t, b, name, kind):
                take(t, name)
                ge(act, shift_in[kind], b * 16)
                nc.scalar.activation(shiftT[:, kind, :], misc[0:H, 0:T], ACT.Copy, scale=-1.0).then_inc(misc_free, 1)

            def evacuate_pv(b, i):
                act.wait_ge(pv_done, b * 8 + 2 * i + 2)
                if i >= 2:
                    ge(act, misc_ready, misc_batch_number(b, f"y{i - 2}") + 1)
                elif on(b - 1):
                    ge(act, misc_ready, misc_batch_number(b - 1, f"y{i + 2}") + 1)
                nc.scalar.activation(y_raw[:, i % 2, :], pv_bank[:, :], ACT.Copy).then_inc(pv_copied, 1)

            def tick(t, par):
                p1 = 1 - par
                for what, n in order("act", t):
                    if what == "exp" and on(t):
                        act.wait_ge(exp_scores, t * NC2 + n + 1)
                        old = n - NP
                        if old >= 0:
                            act.wait_ge(pv_done, t * 8 + S2_GROUP[old] + 1)
                        else:
                            ge(act, pv_done, (t - 1) * 8 + S2_GROUP[old + NC2] + 1 if not isinstance(t, int) or t > 0 else 0)
                        nc.scalar.activation(probs[:, n % NP, :], exp_bank[n % 2][:, :], ACT.Exp).then_inc(exp_done, 1)
                    elif what == "tanh" and on(t - 1):
                        b = t - 1
                        act.wait_ge(gu_ready, b * NB + n + 1)
                        if n >= 2:
                            act.wait_ge(f_gate_done, b * NB + n - 1)
                        nc.scalar.activation(f_tanh[:, n % 2], gu_bank[n % 2][:, 0:T], ACT.Tanh, scale=0.5).then_inc(f_tanh_done, 1)
                    elif what == "xnT" and on(t + 1):
                        take(t, what)
                        nc.scalar.activation(xnT[:, :], misc[:, 0:T], ACT.Copy).then_inc(misc_free, 1)
                    elif what == "yT" and on(t - 1):
                        take(t, what)
                        nc.scalar.activation(yT[:, :], misc[:, 0:T], ACT.Identity, bias=bias_v[:, :]).then_inc(misc_free, 1)
                    elif what == "qproj" and on(t + 1):
                        take(t, what)
                        if isinstance(t, int) and t == FIRST_TICK:
                            act.wait_ge(scaled, 1)
                        ge(act, q_split, (t + 1) * PARTS)
                        nc.scalar.activation(proj[:, 0, 0:T], misc[:, 0:T], ACT.Identity, bias=bias_q[:, 0:1], scale=SCALE)
                        nc.scalar.activation(proj[:, 0, T:2 * T], misc[:, T:2 * T], ACT.Identity, bias=bias_q[:, 1:2],
                                             scale=SCALE).then_inc(misc_free, 1)
                    elif what == "kproj" and on(t + 1):
                        take(t, what)
                        ge(act, k_split, (t + 1) * PARTS)
                        nc.scalar.activation(proj[:, 1, 0:T], misc[:, 0:T], ACT.Identity, bias=cols_sb[:, 2:3])
                        nc.scalar.activation(proj[:, 1, T:2 * T], misc[:, T:2 * T], ACT.Identity,
                                             bias=cols_sb[:, 3:4]).then_inc(misc_free, 1)
                    elif what == "k_part0" and on(t + 1):
                        act.wait_ge(misc_free, misc_number(t, "kproj") + 1)
                        ge(act, k_stored, (t + 1) * 48)
                        nc.scalar.activation(part[:, 1, 0, :], proj[:, 1, :], ACT.Copy).then_inc(k_split, 1)
                    elif what == "vproj" and on(t + 1):
                        take(t, what)
                        act.wait_ge(v_cleared, 1)
                        for kind in (SELF, CROSS):
                            last = nc.scalar.activation(
                                v_ext[:, p1, kind, :, :, 0:D],
                                misc[:, kind * T:(kind + 1) * T].rearrange("p (n h d) -> p n h d", n=NQ, d=D), ACT.Copy)
                        last.then_inc(misc_free, 1)
                    elif what == "xn2T" and on(t - 1):
                        take(t, what)
                        nc.scalar.activation(xn2T[:, :], misc[:, 0:T], ACT.Copy).then_inc(misc_free, 1)
                    elif what == "logits" and on(t - 1):
                        take(t, what)
                        nc.scalar.activation(r_tanh[:, :, :], misc[:, 0:NQ * E].rearrange("p (n e) -> p n e", n=NQ), ACT.Tanh,
                                             scale=0.5).then_inc(misc_free, 1)
                    elif what == "combT" and on(t - 1):
                        take(t, what)
                        nc.scalar.activation(combT[:, :], misc[0:E, 0:T], ACT.Copy).then_inc(misc_free, 1)
                    elif what == "q_part0" and on(t + 1):
                        act.wait_ge(misc_free, misc_number(t, "qproj") + 1)
                        ge(act, q_stored, (t + 1) * 48)
                        nc.scalar.activation(part[:, 0, 0, :], proj[:, 0, :], ACT.Copy).then_inc(q_split, 1)
                    elif what == "shift_self" and on(t):
                        shift(t, t, what, SELF)
                    elif what == "shift_cross" and on(t + 1):
                        shift(t, t + 1, what, CROSS)
                    elif what == "pv_copy" and on(t):
                        evacuate_pv(t, n)

            ticks(act, tick)

        @block.tensor
        def _(pe):
            pe.wait_ge(w_first, 48)
            pe.wait_ge(const_made, 3)

            def max_chunk(b, par, k):
                kind, qt, h0, nh, keys = S1_CHUNKS[k]
                if k == 0:
                    pe.wait_ge(shift_cleared, b * 16 + 16)
                if k in (0, CROSS_C1):
                    pe.wait_ge(stack_in[kind], b * 64 + 64)
                if k == 0:
                    if isinstance(b, int) and b < 2:
                        pe.wait_ge(ones_in, 16 * b + 16)
                ge(pe, max_taken, b * NC1 + k - 1)
                ps = max_bank[k % 2][:, :].rearrange("p (h k) -> p h k", h=nh)
                if kind == SELF:
                    pe.matmul(ps[:, :, keys - 128:keys], ident_b[:, :], causal[:, 0:nh, :], start=True, stop=False)
                for n in range(nh):
                    h = h0 + n
                    q = q_stack[:, par, kind, h, qt * 128:(qt + 1) * 128]
                    if kind == SELF:
                        for kt in range(keys // 128):
                            last = pe.matmul(ps[:, n, kt * 128:(kt + 1) * 128], q, k_stack[:, par, kind, h, kt * 128:(kt + 1) * 128],
                                             start=False, stop=n == nh - 1 and kt == keys // 128 - 1)
                    else:
                        last = pe.matmul(ps[:, n, :], q, k_stack[:, par, kind, h, :], start=n == 0, stop=n == nh - 1)
                last.then_inc(max_scores, 1)

            def exp_chunk(t, par, s):
                kind, kt, h0, nh, q0 = S2_CHUNKS[s]
                if s in (0, CROSS_C2):
                    pe.wait_ge(shift_in[kind], t * 16 + 16)
                ge(pe, exp_done, t * NC2 + s - 1)
                ps = exp_bank[s % 2][:, :].rearrange("p (h q) -> p h q", h=nh)
                for n in range(nh):
                    h = h0 + n
                    last = pe.matmul(ps[:, n, :], k_stack[:, par, kind, h, kt * 128:(kt + 1) * 128],
                                     q_stack[:, par, kind, h, q0:T], start=n == 0, stop=n == nh - 1)
                last.then_inc(exp_scores, 1)

            def weigh_values(t, par, g):
                kind, g4 = (CROSS, SELF)[g // 4], g % 4
                pe.wait_ge(exp_done, t * NC2 + LAST_CHUNK[g] + 1)
                if kind == SELF:
                    pe.wait_ge(mask_done, t * SELF_C2 + 3 * g4 + 3)
                if g % 2 == 0:
                    ge(pe, pv_copied, t * 4 + g // 2)
                col = (g % 2) * T
                for kt in range(NQ):
                    for n in range(4):
                        chunk, at = [(c, h0) for c, (kd, k_, h0, nh, q0) in enumerate(S2_CHUNKS)
                                     if kd == kind and k_ == kt and h0 <= 4 * g4 + n < h0 + nh][0]
                        nh, q0 = S2_CHUNKS[chunk][3:]
                        p = probs[:, chunk % NP, :].rearrange("p (h q) -> p h q", h=nh)[:, 4 * g4 + n - at, :]
                        last = pe.matmul(pv_bank[32 * n:32 * n + VW, col + q0:col + T], v_ext[:, par, kind, kt, 4 * g4 + n, :], p,
                                         start=kt == 0, stop=kt == NQ - 1, tile_position=(0, 32 * n))
                last.then_inc(pv_done, 1)

            def own(t, name):
                ge(pe, misc_free, misc_number(t, name))

            def transposes(dst, src):
                for n in range(NQ):
                    last = pe.transpose(dst[:, n * 128:(n + 1) * 128], src(n), ident[:, :])
                return last

            def misc_use(t, par, name, off):
                b, p1 = t + off, 1 - par
                own(t, name)
                if name == "xnT":
                    pe.wait_ge(xn_done, b + 1)
                    last = transposes(misc, lambda n: xn[:, n, :])
                elif name == "qproj":
                    pe.wait_ge(misc_free, misc_number(t, "xnT") + 1)
                    pe.matmul(misc[:, 0:T], w_q, xnT[:, :], start=True, stop=True)
                    last = pe.matmul(misc[:, T:2 * T], w_cq, xnT[:, :], start=True, stop=True)
                elif name == "kproj":
                    pe.wait_ge(x_loaded, b * 32 + 32)
                    pe.matmul(misc[:, 0:T], w_k, xnT[:, :], start=True, stop=True)
                    last = pe.matmul(misc[:, T:2 * T], w_ck, ctx_in[:, p1, :], start=True, stop=True)
                elif name == "vproj":
                    for n in range(NQ):
                        pe.matmul(misc[:, n * 128:(n + 1) * 128], xnT[:, n * 128:(n + 1) * 128], w_v, start=True, stop=True)
                    for n in range(NQ):
                        last = pe.matmul(misc[:, T + n * 128:T + (n + 1) * 128], ctx_in[:, p1, n * 128:(n + 1) * 128], w_cv,
                                         start=True, stop=True)
                elif name in ("shift_cross", "shift_self"):
                    kind = CROSS if name == "shift_cross" else SELF
                    pe.wait_ge(max_taken, b * NC1 + (CROSS_C1 if kind == CROSS else NC1))
                    for n in range(NQ):
                        last = pe.transpose(misc[0:H, n * 128:(n + 1) * 128], row_max[:, kind, n, :], ident[:, :])
                elif name in ("y0", "y1", "y2", "y3"):
                    i = int(name[1])
                    pe.wait_ge(pv_copied, b * 4 + i + 1)
                    for qt in range(NQ):
                        for g in range(2):
                            last = pe.transpose(misc[:, (qt * 2 + g) * 128:(qt * 2 + g + 1) * 128],
                                                y_raw[:, i % 2, g * T + qt * 128:g * T + (qt + 1) * 128], ident[:, :])
                elif name == "yT":
                    pe.wait_ge(y_done, b + 1)
                    last = transposes(misc, lambda n: y[:, n, :])
                elif name == "wp":
                    pe.wait_ge(misc_free, misc_number(t, "yT") + 1)
                    for n in range(NQ):
                        last = pe.matmul(misc[:, n * 128:(n + 1) * 128], yT[:, n * 128:(n + 1) * 128], w_p, start=True, stop=True)
                elif name == "xn2T":
                    pe.wait_ge(xn2_done, b + 1)
                    last = transposes(misc, lambda n: xn2[:, n, :])
                elif name == "logits":
                    pe.wait_ge(misc_free, misc_number(t, "xn2T") + 1)
                    for n in range(NQ):
                        last = pe.matmul(misc[:, n * E:(n + 1) * E], xn2T[:, n * 128:(n + 1) * 128], w_router, start=True, stop=True)
                elif name == "combT":
                    pe.wait_ge(comb_done, b + 1)
                    for n in range(NQ):
                        last = pe.transpose(misc[0:E, n * 128:(n + 1) * 128], r_w[:, n, :], ident[:, :])
                elif name == "down":
                    for j in range(NB):
                        pe.wait_ge(f_hc_done, b * NB + j + 1)
                        for n in range(NQ):
                            last = pe.matmul(misc[:, n * 128:(n + 1) * 128], f_hc[:, j, n * 128:(n + 1) * 128], w_down[:, j, :],
                                             start=j == 0 and n == 0, stop=j == NB - 1 and n == NQ - 1)
                last.then_inc(misc_ready, 1)

            def gate_up(b, j):
                if j >= 2:
                    pe.wait_ge(f_h_done, b * NB + j - 1)
                e0 = slice(j * 128, (j + 1) * 128)
                pe.matmul(gu_bank[j % 2][:, 0:T], w_gate[:, e0], xn2T[:, :], start=True, stop=True)
                pe.matmul(gu_bank[j % 2][:, T:2 * T], w_up[:, e0], xn2T[:, :], start=True, stop=True).then_inc(gu_ready, 1)

            def tick(t, par):
                for what, n in order("pe", t):
                    if what == "max":
                        off = 0 if n >= CROSS_C1 else 1
                        if on(t + off):
                            max_chunk(t + off, (par + off) % 2, n)
                    elif what == "exp" and on(t):
                        exp_chunk(t, par, n)
                    elif what == "pv" and on(t):
                        weigh_values(t, par, n)
                    elif what == "gate_up" and on(t - 1):
                        gate_up(t - 1, n)
                    elif what in MISC_BATCH and on(t + MISC_BATCH[what]):
                        misc_use(t, par, what, MISC_BATCH[what])
                if isinstance(t, int) and t == FIRST_TICK:
                    pe.wait_ge(w_experts, 32)

            ticks(pe, tick)

        @block.vector
        def _(dve):
            for pads in (r_gin, r_gtop, r_ein, r_etop):
                nc.vector.memset(pads[:, :, :], PAD)

            def scale_constants():
                dve.wait_ge(w_first, 48)
                nc.vector.tensor_scalar(bias_q[:, :], cols_sb[:, 0:2], SCALE, None, ALU.mult)
                nc.vector.tensor_tensor(bias_v[:, :], cols_sb[:, 4:5], cols_sb[:, 5:6], ALU.add).then_inc(scaled, 1)
                dve.wait_ge(gate_made, 1)
                nc.vector.tensor_scalar(gate[:, 2:3], gate[:, 1:2], ROUTED_SCALE / 2, None, ALU.mult).then_inc(gate_made, 1)
                nc.vector.tensor_scalar(bp_row[:, :], rows_sb[:, 0:C], gate[:, 0:1], None, ALU.mult).then_inc(gate_made, 1)

            def clear_stack(st, n, kind):
                words = st[64:128, n, kind].rearrange("p h t -> p (h t)").bitcast(mybir.dt.uint32)
                nc.vector.memset(words, 0).then_inc(stack_cleared, 1)

            def stats(src, st, mv, step, done):
                for n in range(NQ):
                    nc.vector.bn_stats(st[:, n, :], src[:, n, :]).then_inc(step, 1)
                dve.wait_ge(step, NQ)
                dve.sem_clear(step)
                for n in range(NQ):
                    last = nc.vector.bn_aggr(mv[:, n, :], st[:, n, :])
                last.then_inc(done, 1)

            def normalise(src, mv, rs, dst, done):
                for n in range(NQ):
                    last = nc.vector.tensor_scalar(dst[:, n, :], src[:, n, :], mv[:, n, 0:1], rs[:, n:n + 1], ALU.subtract, ALU.mult)
                last.then_inc(done, 1)

            def take_max(b, k):
                kind, qt, h0, nh, keys = S1_CHUNKS[k]
                dve.wait_ge(max_scores, b * NC1 + k + 1)
                nc.vector.tensor_reduce(row_max[:, kind, qt, h0:h0 + nh], max_bank[k % 2][:, :].rearrange("p (h k) -> p h k", h=nh),
                                        AX.X, ALU.max).then_inc(max_taken, 1)

            def merge(t, b, i):
                dve.wait_ge(misc_ready, misc_number(t, f"y{i}") + 1)
                v = misc[:, :].rearrange("p (a v) -> p a v", v=VW)
                nc.vector.reciprocal(recip[:, :].unsqueeze(2), v[:, :, SUM_COL:SUM_COL + 1]).then_inc(y_step, 1)
                dve.wait_ge(y_step, 1)
                dve.sem_clear(y_step)
                half = slice((i % 2) * C // 2, (i % 2 + 1) * C // 2)
                r = recip[:, :].unsqueeze(2).broadcast_to([128, 16, D])
                if i < 2:
                    if i == 0:
                        ge(dve, misc_ready, misc_batch_number(b - 1, "yT") + 1 if not isinstance(b, int) or b > 0 else 0)
                    o = y[:, :, half].rearrange("p n (a d) -> p n a d", d=D)
                    nc.vector.tensor_tensor(o, v[:, :, 0:D].rearrange("p (n a) d -> p n a d", n=NQ),
                                            r.rearrange("p (n a) d -> p n a d", n=NQ), ALU.mult).then_inc(misc_free, 1)
                else:
                    nc.vector.tensor_tensor(y_tmp[:, :, :].rearrange("p n (a d) -> p (n a) d", d=D), v[:, :, 0:D], r,
                                            ALU.mult).then_inc(misc_free, 1)
                    dve.wait_ge(misc_free, misc_number(t, f"y{i}") + 1)
                    last = nc.vector.tensor_tensor(y[:, :, half], y[:, :, half], y_tmp[:, :, :], ALU.add)
                    if i == 3:
                        last.then_inc(y_done, 1)

            def first_stats(b, p):
                dve.wait_ge(x_loaded, b * 32 + 32)
                stats(x_in[:, p], stats1, mean1, ln1_step, stats_done)

            def split_queries(t, b, n):
                src, rem, prt = proj[:, 0, :], rest[:, 0, :], part[:, 0]
                if n == 1:
                    dve.wait_ge(q_split, b * PARTS + 1)
                    nc.vector.tensor_tensor(rem, src, prt[:, 0, :], ALU.subtract).then_inc(q_rest, 1)
                elif n == 2:
                    dve.wait_ge(q_rest, 1)
                    dve.sem_clear(q_rest)
                    nc.vector.tensor_copy(prt[:, 1, :], rem).then_inc(q_split, 1)
                else:
                    dve.wait_ge(q_split, b * PARTS + 2)
                    nc.vector.tensor_tensor(prt[:, 2, :], rem, prt[:, 1, :], ALU.subtract).then_inc(q_split, 1)

            def route(t, b, n):
                grouped = r_choice[:, :, :].rearrange("p n (g e) -> p (n g) e", g=GROUPS)
                by_group = lambda a: a.rearrange("p n (g e) -> p n g e", g=GROUPS)
                per_expert = lambda a: a.unsqueeze(3).broadcast_to([128, NQ, GROUPS, E // GROUPS])
                if n == 0:
                    dve.wait_ge(misc_free, misc_number(t, "logits") + 1)
                else:
                    dve.wait_ge(route_step, n)
                if n == 0:
                    last = nc.vector.tensor_scalar(r_score[:, :, :], r_tanh[:, :, :], 0.5, 0.5, ALU.mult, ALU.add)
                elif n == 1:
                    last = nc.vector.tensor_tensor(r_choice[:, :, :], r_score[:, :, :], rb_row[:, :].unsqueeze(1).broadcast_to([128, NQ, E]),
                                                   ALU.add)
                elif n == 2:
                    nc.vector.tensor_tensor(r_pair[:, :, 0:3], grouped[:, :, 0:3], grouped[:, :, 1:4], ALU.add)
                    nc.vector.tensor_tensor(r_pair[:, :, 3:5], grouped[:, :, 0:2], grouped[:, :, 2:4], ALU.add)
                    last = nc.vector.tensor_tensor(r_pair[:, :, 5:6], grouped[:, :, 0:1], grouped[:, :, 3:4], ALU.add)
                elif n == 3:
                    last = nc.vector.tensor_reduce(r_gin[:, :, 0:GROUPS], r_pair[:, :, :].rearrange("p (n g) k -> p n g k", n=NQ), AX.X, ALU.max)
                elif n == 4:
                    for m in range(NQ):
                        last = nc.vector.max(r_g8[:, m, :], r_gin[:, m, :])
                elif n == 5:
                    last = nc.vector.tensor_copy(r_gtop[:, :, 0:TOP_GROUPS], r_g8[:, :, 0:TOP_GROUPS])
                elif n == 6:
                    for m in range(NQ):
                        last = nc.vector.match_replace(r_gout[:, m, :], r_gtop[:, m, :], r_gin[:, m, :], TAKEN)
                elif n == 7:
                    last = nc.vector.tensor_scalar(r_gsel[:, :, :], r_gout[:, :, 0:GROUPS], TAKEN, None, ALU.is_equal)
                elif n == 8:
                    nc.vector.tensor_scalar(r_gpen[:, :, :], r_gsel[:, :, :], -NEG_INF, NEG_INF, ALU.mult, ALU.add)
                    last = nc.vector.tensor_tensor(by_group(r_ein[:, :, 0:E]), by_group(r_choice[:, :, :]), per_expert(r_gsel[:, :, :]), ALU.mult)
                elif n == 9:
                    o = by_group(r_ein[:, :, 0:E])
                    last = nc.vector.tensor_tensor(o, o, per_expert(r_gpen[:, :, :]), ALU.add)
                elif n == 10:
                    for m in range(NQ):
                        last = nc.vector.max(r_e8[:, m, :], r_ein[:, m, :])
                elif n == 11:
                    last = nc.vector.tensor_copy(r_etop[:, :, 0:TOP_EXPERTS], r_e8[:, :, 0:TOP_EXPERTS])
                elif n == 12:
                    for m in range(NQ):
                        last = nc.vector.match_replace(r_eout[:, m, :], r_etop[:, m, :], r_ein[:, m, :], TAKEN)
                elif n == 13:
                    ge(dve, misc_ready, misc_batch_number(b - 1, "combT") + 1 if not isinstance(b, int) or b > 0 else 0)
                    last = nc.vector.scalar_tensor_tensor(out=r_sel[:, :, :], in0=r_eout[:, :, 0:E], scalar=TAKEN, in1=r_score[:, :, :],
                                                          op0=ALU.is_equal, op1=ALU.mult)
                elif n == 14:
                    last = nc.vector.tensor_reduce(r_sum[:, :], r_sel[:, :, :], AX.X, ALU.add)
                elif n == 15:
                    last = nc.vector.tensor_scalar(r_sum[:, :], r_sum[:, :], 1e-20, None, ALU.add)
                elif n == 16:
                    last = nc.vector.reciprocal(r_sum[:, :], r_sum[:, :])
                else:
                    dve.sem_clear(route_step)
                    nc.vector.scalar_tensor_tensor(out=r_w[:, :, :], in0=r_sel[:, :, :], scalar=gate[:, 2:3],
                                                   in1=r_sum[:, :].unsqueeze(2).broadcast_to([128, NQ, E]),
                                                   op0=ALU.mult, op1=ALU.mult).then_inc(comb_done, 1)
                if n < ROUTE_STEPS - 1:
                    last.then_inc(route_step, 1)

            def swish(b, j):
                dve.wait_ge(f_tanh_done, b * NB + j + 1)
                nc.vector.scalar_tensor_tensor(out=f_gate[:, j % 2], in0=f_tanh[:, j % 2], scalar=1.0, in1=gu_bank[j % 2][:, 0:T],
                                               op0=ALU.add, op1=ALU.mult).then_inc(f_gate_done, 1)

            def times_up(b, j):
                dve.wait_ge(f_gate_done, b * NB + j + 1)
                nc.vector.tensor_tensor(f_h[:, j, :], f_gate[:, j % 2], gu_bank[j % 2][:, T:2 * T], ALU.mult).then_inc(f_h_done, 1)

            def tick(t, par):
                for what, n in order("dve", t):
                    if what == "y" and on(t if n < 3 else t - 1):
                        merge(t, t if n < 3 else t - 1, n)
                    elif what == "max":
                        off = 0 if n >= CROSS_C1 else 1
                        if on(t + off):
                            take_max(t + off, n)
                    elif what == "x1" and on(t - 1):
                        dve.wait_ge(misc_ready, misc_number(t, "wp") + 1)
                        dve.wait_ge(res_done, t)
                        nc.vector.scalar_tensor_tensor(out=x1[:, :, :], in0=misc[:, 0:T].rearrange("p (n c) -> p n c", n=NQ),
                                                       scalar=gate[:, 0:1], in1=x_res[:, 1 - par], op0=ALU.mult, op1=ALU.add)\
                            .then_inc(misc_free, 1)
                    elif what == "stats2" and on(t - 1):
                        dve.wait_ge(misc_free, misc_number(t, "wp") + 1)
                        stats(x1, stats2, mean2, ln2_step, stats2_done)
                    elif what == "queries" and on(t + 1):
                        split_queries(t, t + 1, n)
                    elif what == "keys":
                        split_keys(nc.vector, t + 1, n)
                        if n == PARTS:
                            for st in (q_stack, k_stack):
                                for kind in (SELF, CROSS):
                                    clear_stack(st, 1, kind)
                    elif what == "xn2" and on(t - 1):
                        b = t - 1
                        dve.wait_ge(rstd2_done, b + 1)
                        ge(dve, misc_ready, misc_batch_number(b - 1, "xn2T") + 1 if not isinstance(b, int) or b > 0 else 0)
                        normalise(x1, mean2, rstd2, xn2, xn2_done)
                    elif what == "route" and on(t - 1):
                        route(t, t - 1, n)
                    elif what == "swish" and on(t - 1):
                        swish(t - 1, n)
                    elif what == "times_up" and on(t - 1):
                        times_up(t - 1, n)
                    elif what == "stats1" and on(t + 2):
                        first_stats(t + 2, par)
                    elif what == "out" and on(t - 1):
                        dve.wait_ge(misc_ready, misc_number(t, "down") + 1)
                        dve.wait_ge(stored, (t - 1) * 16 + 16)
                        nc.vector.tensor_tensor(y_out[:, :, :], misc[:, 0:T].rearrange("p (n c) -> p n c", n=NQ), x1[:, :, :],
                                                ALU.add).then_inc(misc_free, 1)

            clear_stack(q_stack, 0, CROSS)
            first_stats(0, 0)
            scale_constants()
            clear_stack(q_stack, 0, SELF)
            ticks(dve, tick)


_P = "L0_xattn_"
_F = "L0_ffn_"


def kernel(**inputs):
    import numpy as np
    import concourse.bacc as bacc
    from concourse.bass_utils import run_bass_kernel_spmd

    a = {k: np.asarray(v) for k, v in inputs.items()}
    p = lambda n: a[_P + n]
    by_d = lambda w: w.reshape(w.shape[:-1] + (H, D)).swapaxes(-1, -2).reshape(w.shape)
    ins = {
        "x": a["x"], "ctxT": a["ctx_512"].transpose(2, 0, 1),
        "w_model": np.concatenate([by_d(p("Wq")), by_d(p("Wcq")), by_d(p("Wk")), p("Wv"), p("Wp"), a[_F + "router_weight"].T], axis=1),
        "w_ctx": np.concatenate([by_d(p("Wck")), p("Wcv")], axis=1),
        "cols": np.stack([by_d(p(n)) for n in ("bq", "bcq", "bk", "bck")] + [p("bv"), p("bcv")], axis=1),
        "rows": np.concatenate([p("bp"), a[_F + "router_bias"], a["g_xattn"], a["g_ffn"]]),
        "w_pairs": np.stack([a[_F + n].transpose(2, 0, 1).reshape(C, E * I) for n in ("w_gate", "w_up")], axis=1),
        "w_down": a[_F + "w_down"].transpose(0, 2, 1).reshape(NB, 128, C).transpose(1, 0, 2),
    }
    nc = bacc.Bacc("TRN2", target_bir_lowering=False, num_devices=1)
    arrays, args = {}, []
    for name, v in ins.items():
        v = np.ascontiguousarray(v)
        arrays["in_" + name] = v
        args.append(nc.dram_tensor("in_" + name, v.shape, mybir.dt.from_np(v.dtype), kind="ExternalInput").ap())
    out = nc.dram_tensor("out", (B, T, C), FP32, kind="ExternalOutput").ap()
    build(nc, *args, out)
    r = run_bass_kernel_spmd(nc, [arrays], core_ids=[0])
    return r.results[0]["out"]
```
